# Optimizing a Trainium2 kernel written in Bass

```python
import numpy as np
import jax
import jax.numpy as jnp

def _softmax(x, axis=-1):
    return jax.nn.softmax(x, axis=axis)

def _gelu(x):
    return jax.nn.gelu(x, approximate=True)

def _silu(x):
    return jax.nn.silu(x)

def _sigmoid(x):
    return jax.nn.sigmoid(x)

def _layernorm(x, axis=-1, eps=1e-05):
    m = jnp.mean(x, axis=axis, keepdims=True)
    v = jnp.var(x, axis=axis, keepdims=True)
    return (x - m) / jnp.sqrt(v + eps)

def _scatter_add(tgt, idx, src, axis=0):
    return tgt.at[idx].add(src)

def _segment_sum(src, seg, n):
    return jax.ops.segment_sum(src, seg, n)
kernel_name = 'mk_perceiver_d1_seqx_r2_4b71be'

def setup_inputs(seed: int=0):
    np.random.seed(seed)
    _w = jnp.asarray

    def _rec_inputs():
        import jax
        import jax.numpy as jnp
        _rk = jax.random.key(seed)
        x = -0.0002928 + 1 * jax.random.normal(jax.random.fold_in(_rk, 1), (16, 64, 1024), jnp.float32)
        _lenS = 64 - jax.random.randint(jax.random.fold_in(_rk, 7), (16,), 0, max(1, 64 // 4) + 1, jnp.int32)
        _lenS2 = 512 - jax.random.randint(jax.random.fold_in(_rk, 8), (16,), 0, max(1, 512 // 4) + 1, jnp.int32)
        _ctx_512P = jax.random.normal(jax.random.fold_in(_rk, 11), (16, 16, 256), jnp.float32)
        _ctx_512c = jax.random.dirichlet(jax.random.fold_in(_rk, 511), 0.3 * jnp.ones((16,), jnp.float32), (16, 512))
        _ctx_512t = jnp.einsum('bsk,bkd->bsd', _ctx_512c, _ctx_512P)
        _ctx_512t = _ctx_512t * jax.lax.rsqrt(jnp.mean(jnp.square(_ctx_512t)) + 1e-12) * 0.953939
        ctx_512 = 0.000227908 + 0.99994 * (_ctx_512t + 0.3 * jax.random.normal(jax.random.fold_in(_rk, 611), (16, 512, 256), jnp.float32))
        return (x, ctx_512)
    x, ctx_512 = _rec_inputs()

    def _L0_xattn_setup():
        import jax, jax.numpy as jnp
        import numpy as np
        B, S, L = (2, 512, 512)
        DIM_Q, H, K, D_C, D_CQ, R = (1024, 16, 128, 256, 768, 64)

        def _rope_tables(length, dim):
            inv = 1.0 / 10000.0 ** (jnp.arange(0, dim, 2, dtype=jnp.float32) / dim)
            f = jnp.arange(length, dtype=jnp.float32)[:, None] * inv[None, :]
            sin = jnp.repeat(jnp.sin(f), 2, axis=-1)
            cos = jnp.repeat(jnp.cos(f), 2, axis=-1)
            return (sin, cos)

        def _rotate_half(x):
            half = x.shape[-1] // 2
            return jnp.concatenate([-x[..., half:], x[..., :half]], axis=-1)

        def _apply_rope(x, sin, cos):
            return x * cos + _rotate_half(x) * sin
        key = jax.random.key(seed)
        ks = jax.random.split(key, 8)
        return {'hidden_q': jax.random.normal(ks[0], (B, S, DIM_Q), jnp.float32), 'kv_c': jax.random.normal(ks[1], (B, L, D_C), jnp.float32), 'Wq': jax.random.normal(ks[2], (H * K, DIM_Q), jnp.float32) / np.sqrt(DIM_Q).astype(np.float32), 'w_kc_q': jax.random.normal(ks[3], (H, K, D_CQ), jnp.float32) / np.sqrt(K).astype(np.float32), 'w_kc_kv': jax.random.normal(ks[4], (H, K, D_C), jnp.float32) / np.sqrt(K).astype(np.float32), 'W_qr': jax.random.normal(ks[5], (H, D_CQ, R), jnp.float32) / np.float32(np.sqrt(D_CQ) * np.sqrt(R)), 'W_kr': jax.random.normal(ks[6], (H, D_C, R), jnp.float32) / np.sqrt(D_C).astype(np.float32), 'Wo': jax.random.normal(ks[7], (DIM_Q, H * K), jnp.float32) / np.sqrt(H * K).astype(np.float32)}
    _L0_xattn_all = _L0_xattn_setup()
    _L0_xattn_in = {k: v for k, v in _L0_xattn_all.items() if k in ('Wq', 'w_kc_q', 'w_kc_kv', 'W_qr', 'W_kr', 'Wo')}
    del _L0_xattn_all

    def _L0_attn_setup():
        import jax, jax.numpy as jnp
        import numpy as np
        from functools import partial
        H = 1024
        NH = 16
        HD = 128
        K = 4
        EPS = 1e-05

        def short_conv_silu(x, w):
            s = x.shape[1]
            xp = jnp.pad(x, ((0, 0), (K - 1, 0), (0, 0)))
            y = sum((xp[:, i:i + s, :] * w[:, i] for i in range(K)))
            return jax.nn.silu(y)

        def l2norm(x):
            return x * jax.lax.rsqrt(jnp.sum(x * x, axis=-1, keepdims=True) + 1e-12)

        def delta_rule(q, k, v, beta):
            d = q.shape[-1]
            q = l2norm(q) * d ** (-0.5)
            k = l2norm(k)
            qs, ks, vs = (jnp.moveaxis(t, 1, 0) for t in (q, k, v))
            bs = jnp.moveaxis(beta, 1, 0)
            b, h = (q.shape[0], q.shape[2])
            S0 = jnp.zeros((b, h, d, d), dtype=q.dtype)

            def step(S, inp):
                qt, kt, vt, bt = inp
                v_pred = jnp.einsum('bhk,bhkv->bhv', kt, S)
                u = bt[..., None] * (vt - v_pred)
                S = S + jnp.einsum('bhk,bhv->bhkv', kt, u)
                o = jnp.einsum('bhk,bhkv->bhv', qt, S)
                return (S, o)
            _, os = jax.lax.scan(step, S0, (qs, ks, vs, bs))
            return jnp.moveaxis(os, 0, 1)

        def deltanet_forward(hidden_states, Wq, Wk, Wv, Wb, conv_q, conv_k, conv_v, g_norm, Wo):
            q = jnp.einsum('sbh,hc->bsc', hidden_states, Wq)
            k = jnp.einsum('sbh,hc->bsc', hidden_states, Wk)
            v = jnp.einsum('sbh,hc->bsc', hidden_states, Wv)
            hs_bsh = jnp.swapaxes(hidden_states, 0, 1)
            q = short_conv_silu(q, conv_q)
            k = short_conv_silu(k, conv_k)
            v = short_conv_silu(v, conv_v)
            b, s = (q.shape[0], q.shape[1])
            q = q.reshape(b, s, NH, HD)
            k = k.reshape(b, s, NH, HD)
            v = v.reshape(b, s, NH, HD)
            beta = jax.nn.sigmoid(jnp.einsum('bsh,hn->bsn', hs_bsh, Wb))
            o = delta_rule(q, k, v, beta)
            o = o * jax.lax.rsqrt(jnp.mean(o * o, axis=-1, keepdims=True) + EPS) * g_norm
            o = o.reshape(b, s, NH * HD)
            o = jnp.einsum('bsc,ch->sbh', o, Wo)
            return o
        key = jax.random.key(seed)
        ks = jax.random.split(key, 10)
        S, B = (1024, 2)
        C = NH * HD
        inp = {'hidden_states': jax.random.normal(ks[0], (S, B, H), dtype=jnp.float32), 'Wq': jax.random.normal(ks[1], (H, C), dtype=jnp.float32) * 0.02, 'Wk': jax.random.normal(ks[2], (H, C), dtype=jnp.float32) * 0.02, 'Wv': jax.random.normal(ks[3], (H, C), dtype=jnp.float32) * 0.02, 'Wb': jax.random.normal(ks[4], (H, NH), dtype=jnp.float32) * 0.02, 'conv_q': jax.random.normal(ks[5], (C, K), dtype=jnp.float32) * 0.5, 'conv_k': jax.random.normal(ks[6], (C, K), dtype=jnp.float32) * 0.5, 'conv_v': jax.random.normal(ks[7], (C, K), dtype=jnp.float32) * 0.5, 'g_norm': jnp.ones((HD,), dtype=jnp.float32), 'Wo': jax.random.normal(ks[8], (C, H), dtype=jnp.float32) * 0.02}
        return inp
    _L0_attn_all = _L0_attn_setup()
    _L0_attn_in = {k: v for k, v in _L0_attn_all.items() if k in ('Wq', 'Wk', 'Wv', 'Wb', 'conv_q', 'conv_k', 'conv_v', 'g_norm', 'Wo')}
    del _L0_attn_all

    def _L0_ffn_setup():
        import jax, jax.numpy as jnp
        import numpy as np
        B, P = (32, 128)
        DIMS = [1024, 2048, 2048, 1024]
        key = jax.random.key(seed)
        ks = jax.random.split(key, 7)

        def lin(k, fan_out, fan_in):
            s = 1.0 / np.sqrt(fan_in)
            return jax.random.uniform(k, (fan_out, fan_in), jnp.float32, -s, s)
        return {'classifier_input': jax.random.normal(ks[0], (B, P, DIMS[0]), jnp.float32), 'W1': lin(ks[1], DIMS[1], DIMS[0]), 'b1': jax.random.uniform(ks[2], (DIMS[1],), jnp.float32, -0.02, 0.02), 'W2': lin(ks[3], DIMS[2], DIMS[1]), 'b2': jax.random.uniform(ks[4], (DIMS[2],), jnp.float32, -0.02, 0.02), 'W3': lin(ks[5], DIMS[3], DIMS[2]), 'b3': jax.random.uniform(ks[6], (DIMS[3],), jnp.float32, -0.02, 0.02)}
    _L0_ffn_all = _L0_ffn_setup()
    _L0_ffn_in = {k: v for k, v in _L0_ffn_all.items() if k in ('W1', 'b1', 'W2', 'b2', 'W3', 'b3')}
    del _L0_ffn_all
    return {'x': x, 'ctx_512': ctx_512, 'L0_xattn_Wq': _L0_xattn_in['Wq'], 'L0_xattn_w_kc_q': _L0_xattn_in['w_kc_q'], 'L0_xattn_w_kc_kv': _L0_xattn_in['w_kc_kv'], 'L0_xattn_W_qr': _L0_xattn_in['W_qr'], 'L0_xattn_W_kr': _L0_xattn_in['W_kr'], 'L0_xattn_Wo': _L0_xattn_in['Wo'], 'L0_attn_Wq': _L0_attn_in['Wq'], 'L0_attn_Wk': _L0_attn_in['Wk'], 'L0_attn_Wv': _L0_attn_in['Wv'], 'L0_attn_Wb': _L0_attn_in['Wb'], 'L0_attn_conv_q': _L0_attn_in['conv_q'], 'L0_attn_conv_k': _L0_attn_in['conv_k'], 'L0_attn_conv_v': _L0_attn_in['conv_v'], 'L0_attn_g_norm': _L0_attn_in['g_norm'], 'L0_attn_Wo': _L0_attn_in['Wo'], 'L0_ffn_W1': _L0_ffn_in['W1'], 'L0_ffn_b1': _L0_ffn_in['b1'], 'L0_ffn_W2': _L0_ffn_in['W2'], 'L0_ffn_b2': _L0_ffn_in['b2'], 'L0_ffn_W3': _L0_ffn_in['W3'], 'L0_ffn_b3': _L0_ffn_in['b3']}

def reference(x, ctx_512, L0_xattn_Wq, L0_xattn_w_kc_q, L0_xattn_w_kc_kv, L0_xattn_W_qr, L0_xattn_W_kr, L0_xattn_Wo, L0_attn_Wq, L0_attn_Wk, L0_attn_Wv, L0_attn_Wb, L0_attn_conv_q, L0_attn_conv_k, L0_attn_conv_v, L0_attn_g_norm, L0_attn_Wo, L0_ffn_W1, L0_ffn_b1, L0_ffn_W2, L0_ffn_b2, L0_ffn_W3, L0_ffn_b3):
    import jax
    import jax.numpy as jnp

    def _L0_xattn_ref(hidden_q, kv_c, Wq, w_kc_q, w_kc_kv, W_qr, W_kr, Wo):
        import jax, jax.numpy as jnp
        import numpy as np
        B, S, L = (2, 512, 512)
        DIM_Q, H, K, D_C, D_CQ, R = (1024, 16, 128, 256, 768, 64)

        def _rope_tables(length, dim):
            inv = 1.0 / 10000.0 ** (jnp.arange(0, dim, 2, dtype=jnp.float32) / dim)
            f = jnp.arange(length, dtype=jnp.float32)[:, None] * inv[None, :]
            sin = jnp.repeat(jnp.sin(f), 2, axis=-1)
            cos = jnp.repeat(jnp.cos(f), 2, axis=-1)
            return (sin, cos)

        def _rotate_half(x):
            half = x.shape[-1] // 2
            return jnp.concatenate([-x[..., half:], x[..., :half]], axis=-1)

        def _apply_rope(x, sin, cos):
            return x * cos + _rotate_half(x) * sin
        Bv, Sv, _ = hidden_q.shape
        _, Lv, _ = kv_c.shape
        q_hk = (hidden_q @ Wq.T).reshape(Bv, Sv, H, K)
        q_big = jnp.einsum('bshk,hkq->bshq', q_hk, w_kc_q)
        sin_q, cos_q = _rope_tables(Sv, D_CQ)
        q_big = _apply_rope(q_big, sin_q[None, :, None, :], cos_q[None, :, None, :])
        sin_k, cos_k = _rope_tables(Lv, D_C)
        kv_r = _apply_rope(kv_c, sin_k[None], cos_k[None])
        q_r = jnp.einsum('bshq,hqr->bhsr', q_big, W_qr)
        k_r = jnp.einsum('bld,hdr->bhlr', kv_r, W_kr)
        scores = jnp.einsum('bhsr,bhlr->bhsl', q_r, k_r)
        attn = jax.nn.softmax(scores, axis=-1)
        ctx_c = jnp.einsum('bhsl,bld->bhsd', attn, kv_r)
        ctx_lat = jnp.einsum('bhsd,hkd->bhsk', ctx_c, w_kc_kv)
        ctx = ctx_lat.transpose(0, 2, 1, 3).reshape(Bv, Sv, H * K)
        return ctx @ Wo.T

    def _L0_attn_ref(hidden_states, Wq, Wk, Wv, Wb, conv_q, conv_k, conv_v, g_norm, Wo):
        import jax, jax.numpy as jnp
        import numpy as np
        from functools import partial
        H = 1024
        NH = 16
        HD = 128
        K = 4
        EPS = 1e-05

        def short_conv_silu(x, w):
            s = x.shape[1]
            xp = jnp.pad(x, ((0, 0), (K - 1, 0), (0, 0)))
            y = sum((xp[:, i:i + s, :] * w[:, i] for i in range(K)))
            return jax.nn.silu(y)

        def l2norm(x):
            return x * jax.lax.rsqrt(jnp.sum(x * x, axis=-1, keepdims=True) + 1e-12)

        def delta_rule(q, k, v, beta):
            d = q.shape[-1]
            q = l2norm(q) * d ** (-0.5)
            k = l2norm(k)
            qs, ks, vs = (jnp.moveaxis(t, 1, 0) for t in (q, k, v))
            bs = jnp.moveaxis(beta, 1, 0)
            b, h = (q.shape[0], q.shape[2])
            S0 = jnp.zeros((b, h, d, d), dtype=q.dtype)

            def step(S, inp):
                qt, kt, vt, bt = inp
                v_pred = jnp.einsum('bhk,bhkv->bhv', kt, S)
                u = bt[..., None] * (vt - v_pred)
                S = S + jnp.einsum('bhk,bhv->bhkv', kt, u)
                o = jnp.einsum('bhk,bhkv->bhv', qt, S)
                return (S, o)
            _, os = jax.lax.scan(step, S0, (qs, ks, vs, bs))
            return jnp.moveaxis(os, 0, 1)

        def deltanet_forward(hidden_states, Wq, Wk, Wv, Wb, conv_q, conv_k, conv_v, g_norm, Wo):
            q = jnp.einsum('sbh,hc->bsc', hidden_states, Wq)
            k = jnp.einsum('sbh,hc->bsc', hidden_states, Wk)
            v = jnp.einsum('sbh,hc->bsc', hidden_states, Wv)
            hs_bsh = jnp.swapaxes(hidden_states, 0, 1)
            q = short_conv_silu(q, conv_q)
            k = short_conv_silu(k, conv_k)
            v = short_conv_silu(v, conv_v)
            b, s = (q.shape[0], q.shape[1])
            q = q.reshape(b, s, NH, HD)
            k = k.reshape(b, s, NH, HD)
            v = v.reshape(b, s, NH, HD)
            beta = jax.nn.sigmoid(jnp.einsum('bsh,hn->bsn', hs_bsh, Wb))
            o = delta_rule(q, k, v, beta)
            o = o * jax.lax.rsqrt(jnp.mean(o * o, axis=-1, keepdims=True) + EPS) * g_norm
            o = o.reshape(b, s, NH * HD)
            o = jnp.einsum('bsc,ch->sbh', o, Wo)
            return o
        return deltanet_forward(hidden_states, Wq, Wk, Wv, Wb, conv_q, conv_k, conv_v, g_norm, Wo)

    def _L0_ffn_ref(classifier_input, W1, b1, W2, b2, W3, b3):
        import jax, jax.numpy as jnp
        import numpy as np
        B, P = (32, 128)
        DIMS = [1024, 2048, 2048, 1024]
        x = classifier_input
        x = jax.nn.relu(jnp.einsum('bpd,hd->bph', x, W1) + b1)
        x = jax.nn.relu(jnp.einsum('bpd,hd->bph', x, W2) + b2)
        out = jnp.einsum('bpd,od->bpo', x, W3) + b3
        return out
    x = x + _L0_xattn_ref(_layernorm(x, axis=-1), ctx_512, L0_xattn_Wq, L0_xattn_w_kc_q, L0_xattn_w_kc_kv, L0_xattn_W_qr, L0_xattn_W_kr, L0_xattn_Wo)
    x = x + _L0_attn_ref(_layernorm(x, axis=-1), L0_attn_Wq, L0_attn_Wk, L0_attn_Wv, L0_attn_Wb, L0_attn_conv_q, L0_attn_conv_k, L0_attn_conv_v, L0_attn_g_norm, L0_attn_Wo)
    x = x + _L0_ffn_ref(_layernorm(x, axis=-1), L0_ffn_W1, L0_ffn_b1, L0_ffn_W2, L0_ffn_b2, L0_ffn_W3, L0_ffn_b3)
    return x

_drawn_inputs = setup_inputs


def setup_inputs(seed=0):
    import zlib

    import numpy as np

    out = dict(_drawn_inputs(seed))
    spreads = {'L0_attn_g_norm': (1.0, 0.2)}
    factors = {'L0_ffn_b1': 39.088, 'L0_ffn_b2': 8.0, 'L0_ffn_b3': 6.239}
    for name, (base, spread) in spreads.items():
        noise = np.random.default_rng([zlib.crc32(name.encode()), seed]).standard_normal(out[name].shape)
        drawn = base * np.exp(spread * noise) if base else spread * noise
        out[name] = jnp.asarray(drawn.astype(out[name].dtype))
    for name, factor in factors.items():
        out[name] = (out[name] * factor).astype(out[name].dtype)
    return out
```

```python
from contextlib import ExitStack

import concourse.bass as bass
from concourse import mybir

F32 = mybir.dt.float32
F16 = mybir.dt.float16
ALU = mybir.AluOpType
ACT = mybir.ActivationFunctionType
AXX = mybir.AxisListType.X

P = 128
TOK = 1024
HALF = 512
DM = 1024
KC = DM // P
H = 16
NB = 16
S = 64
L = 512
DC = 256
CQ = 768
CJ = CQ // P
R = 64
T = 16
DB = 64
G8 = 8
W_SCALE = 256.0
QR_SCALE = 16.0
PR_SCALE = 4096.0
LN_EPS = 1e-5
KB = 1024

GEMMS = [("xq", 16, 1), ("xo", 8, 2), ("dk", 16, 1), ("dq", 16, 1), ("dv", 16, 1), ("do", 8, 2),
         ("f1", 16, 1), ("f2", 16, 2), ("f3", 8, 2)]
UNIT0, n = {}, 0
for name, chunks, per in GEMMS:
    UNIT0[name] = n
    n += chunks * per
UNITS = n


def one(ap):
    return ap.rearrange("p a n -> p (a n)")


def build(nc, io):
    ctx = ExitStack()
    with ctx:
        def sem(name):
            return ctx.enter_context(nc.semaphore(name))

        xid = ctx.enter_context(nc.sbuf_tensor("ident_sb", [P, P], F32))
        xones = ctx.enter_context(nc.sbuf_tensor("ones_sb", [P, P], F32))
        same = ctx.enter_context(nc.sbuf_tensor("same_sb", [P, P], F32))
        upto = ctx.enter_context(nc.sbuf_tensor("upto_sb", [P, P], F32))
        vecs = ctx.enter_context(nc.sbuf_tensor("vecs_sb", [P, 256], F32))
        onesm = ctx.enter_context(nc.sbuf_tensor("onesm", [P, 1], F32))
        small = ctx.enter_context(nc.sbuf_tensor("small", [P, 256], F32))
        wst = ctx.enter_context(nc.sbuf_tensor("wst", [P, 2, 1024], F32))
        whi = ctx.enter_context(nc.sbuf_tensor("whi", [P, 2, 1024], F16))
        wlo = ctx.enter_context(nc.sbuf_tensor("wlo", [P, 2, 1024], F16))
        arena = ctx.enter_context(nc.sbuf_tensor("arena", [P, 186 * 256], F32))

        def f32(kb, cols):
            a = int(kb * 256)
            return arena[:, a:a + cols]

        def f16(kb, cols):
            a = int(kb * 256)
            return arena[:, a:a + cols // 2].bitcast(F16)

        def f16c(kb, chunks):
            return f16(kb, chunks * TOK).rearrange("p (c n) -> p c n", n=TOK)

        ps = ctx.enter_context(nc.psum_tensor("ps", [P, 8, HALF], F32))

        def bank(b, k=1):
            return ps[:, b:b + k, :].rearrange("p a n -> p (a n)")

        r0h, r0l = f16c(0, 16), f16c(32, 16)
        xnh, xnl = f16c(64, 8), f16c(80, 8)
        b1c, b2c, b3c = vecs[:, 0:16], vecs[:, 16:32], vecs[:, 32:40]
        gno = vecs[:, 40:41]
        convw = {"dk": vecs[:, 48:112], "dq": vecs[:, 112:176], "dv": vecs[:, 176:240]}

        c_ld = sem("constants_loaded")
        w_ld = [sem("weights_loaded_0"), sem("weights_loaded_1")]
        w_hi = sem("weights_hi")
        w_rdy = sem("weights_split")
        w_used = sem("weights_used")
        acc_rd = sem("accumulator_read")

        def bc(ap, count, axis=1):
            shape = list(ap.shape)
            return ap.unsqueeze(axis).to_broadcast(shape[:axis] + [count] + shape[axis:])

        def load_w(e, u, s):
            e.dma_start(wst[:, s, :], one(io["wstream"][bass.ds(u, 1)].rearrange("a p n -> p a n"))).then_inc(w_ld[s], 16)

        def load_stream(e, u0, u1):
            with e.Fori(u0 // 2, u1 // 2) as i:
                for s in range(2):
                    e.wait_ge(w_rdy, i * 2 + (s - 1))
                    load_w(e, i * 2 + s, s)

        def split_hi(e, u, s, u2, first=False):
            e.wait_ge(w_ld[s], (u2 + 1) * 16)
            if not first:
                e.wait_ge(w_used, u - 1)
            e.activation(whi[:, s, :], wst[:, s, :], ACT.Copy, scale=W_SCALE).then_inc(w_hi, 1)

        def split_lo(e, u, s):
            e.wait_ge(w_hi, u + 1)
            e.scalar_tensor_tensor(out=wlo[:, s, :], in0=wst[:, s, :], scalar=W_SCALE, in1=whi[:, s, :],
                                   op0=ALU.mult, op1=ALU.subtract).then_inc(w_rdy, 1)

        def unit_mm(e, s, dst, sh, sl, k0, ks, first, last, inc):
            mm = None
            for k in ks:
                wh, wl = whi[:, s, k * P:k * P + P], wlo[:, s, k * P:k * P + P]
                for a, (w, x) in enumerate(((wh, sh), (wh, sl), (wl, sh))):
                    for c in range(2):
                        mm = e.matmul(dst[:, c * HALF:(c + 1) * HALF], w, x[:, k0 + k, c * HALF:(c + 1) * HALF],
                                      start=(first and k == ks[0] and a == 0),
                                      stop=(last and k == ks[-1] and a == 2))
            if inc:
                mm.then_inc(w_used, 1)

        PER = {name: per for name, _, per in GEMMS}
        ACC0 = {"xo": 0, "dk": 8, "dq": 24, "dv": 40, "do": 56, "f1": 64, "f2": 80, "f3": 96}

        def acc_done(name, m):
            return m + (ACC0[name] + 3)

        def used(name, m):
            return m * PER[name] + (UNIT0[name] + PER[name])

        def gemm_pe(e, name, m, par, sh, sl, parts=(0, 8)):
            if parts[0] == 0:
                e.wait_ge(acc_rd, m + (ACC0[name] + 1))
            for q in range(PER[name]):
                s = (par * PER[name] + q) % 2
                if parts[0] == 0:
                    e.wait_ge(w_rdy, m * PER[name] + (UNIT0[name] + q + 1))
                unit_mm(e, s, bank(2 * par, 2), sh, sl, q * 8, list(range(*parts)), q == 0 and parts[0] == 0,
                        q == PER[name] - 1 and parts[1] == 8, parts[1] == 8)

        def split_next(e, what, name, m, par, i):
            for q in range(PER[name]):
                s = (par * PER[name] + q) % 2
                u = m * PER[name] + (UNIT0[name] + q + 2)
                if what == "hi":
                    split_hi(e, u, s, (i if PER[name] == 1 else m) + (UNIT0[name] // 2 + 1))
                else:
                    split_lo(e, u, s)

        def pairs(e, n, body, peel=0, peel_end=0):
            def run(i, last):
                for par in range(2):
                    body(i * 2 + par, par, i, last)
            for i in range(peel):
                run(i, False)
            if n // 2 - peel - peel_end > 0:
                with e.Fori(peel, n // 2 - peel_end) as i:
                    run(i, False)
            for i in range(n // 2 - peel_end, n // 2):
                run(i, True)

        lnS, lnQ, lnX, lnM, lnR, lnV = (f32(96 + 4 * k, TOK) for k in range(6))
        lnT = f32(120, 2 * TOK).rearrange("p (c n) -> p c n", n=TOK)
        lnE = f32(128, 2 * TOK).rearrange("p (c n) -> p c n", n=TOK)
        XT = f32(154, KC * TOK).rearrange("p (c n) -> p c n", n=TOK)
        sq_rdy = sem("squares")
        st_s = sem("sum_updated")
        st_q = sem("square_sum_updated")
        ln_mm = sem("ln_means")
        ln_a = sem("ln_scalar_steps")
        ln_v = sem("ln_vector_steps")
        ln_t = sem("ln_centred")
        ln_x = sem("ln_scaled")
        ln_h = sem("ln_hi")
        ln_l = sem("ln_lo")
        LN_OF = {1: "xo", 2: "do"}

        def ln_done(z):
            return 8 * z + 10

        def x_chunk(m):
            return one(XT[:, bass.ds(m, 1), :])

        def ln_square(e, z, m):
            if z:
                e.wait_ge(acc_rd, acc_done(LN_OF[z], m))
            e.wait_ge(st_q, m + (9 * z + 1))
            e.activation(lnX, x_chunk(m), ACT.Square).then_inc(sq_rdy, 1)

        def ln_sum(e, z, m):
            if z:
                e.wait_ge(acc_rd, acc_done(LN_OF[z], m))
            e.wait_ge(st_s, m + (9 * z + 1))
            e.tensor_tensor(lnS, lnS, x_chunk(m), ALU.add).then_inc(st_s, 1)

        def ln_square_sum(e, z, m):
            e.wait_ge(sq_rdy, m + (8 * z + 1))
            e.wait_ge(st_q, m + (9 * z + 1))
            e.tensor_tensor(lnQ, lnQ, lnX, ALU.add).then_inc(st_q, 1)

        def ln_pe(e, z):
            e.wait_ge(st_s, 9 * z + 9)
            e.wait_ge(st_q, 9 * z + 9)
            for b, src in ((4, lnS), (6, lnQ)):
                for c in range(2):
                    mm = e.matmul(bank(b + c), xones[:, :], src[:, c * HALF:(c + 1) * HALF], start=True, stop=True)
            mm.then_inc(ln_mm, 1)

        def ln_act(e, z):
            e.wait_ge(ln_mm, z + 1)
            e.activation(lnM, bank(4, 2), ACT.Copy).then_inc(ln_a, 1)
            e.activation(lnX, bank(4, 2), ACT.Square).then_inc(ln_a, 1)
            e.wait_ge(ln_v, 3 * z + 2)
            e.activation(lnR, lnV, ACT.Sqrt).then_inc(ln_a, 1)

            def chunk(c, s, i, last):
                e.wait_ge(ln_x, c + (8 * z + 3))
                e.activation(one(xnh[:, bass.ds(c, 1), :]), lnE[:, s, :], ACT.Copy).then_inc(ln_h, 1)
            pairs(e, KC, chunk)

        def ln_pool(e, z):
            e.wait_ge(ln_a, 3 * z + 1)

            def chunk(c, s, i, last):
                e.wait_ge(ln_x, c + (8 * z + 1))
                e.tensor_tensor(lnT[:, s, :], x_chunk(c), lnM, ALU.subtract).then_inc(ln_t, 1)
            pairs(e, KC, chunk)

        def ln_dve(e, z):
            e.wait_ge(ln_mm, z + 1)
            e.wait_ge(ln_a, 3 * z + 2)
            e.tensor_tensor(lnV, bank(6, 2), lnX, ALU.subtract).then_inc(ln_v, 1)
            e.wait_ge(ln_v, 3 * z + 1)
            e.tensor_scalar(lnV, lnV, 0.0, LN_EPS, ALU.max, ALU.add).then_inc(ln_v, 1)
            e.wait_ge(ln_a, 3 * z + 3)
            e.reciprocal(lnV, lnR).then_inc(ln_v, 1)
            e.wait_ge(ln_v, 3 * z + 3)

            def chunk(c, s, i, last):
                e.wait_ge(ln_t, c + (8 * z + 1))
                e.wait_ge(ln_l, c + (8 * z + 1))
                e.tensor_tensor(lnE[:, s, :], lnT[:, s, :], lnV, ALU.mult).then_inc(ln_x, 1)
                e.wait_ge(ln_h, c + (8 * z + 1))
                e.tensor_tensor(one(xnl[:, bass.ds(c, 1), :]), lnE[:, s, :], one(xnh[:, bass.ds(c, 1), :]),
                                ALU.subtract).then_inc(ln_l, 1)
            pairs(e, KC, chunk)

        def start_sp(e):
            for c in range(4):
                e.dma_start(XT[:, 2 * c:2 * c + 2, :], io["xT"][:, 2 * c:2 * c + 2, :]).then_inc(x_lds[c], 16)
            load_w(e, 0, 0)
            load_w(e, 1, 1)
            for dst, src in ((xid, "ident"), (xones, "ones"), (same, "same"), (upto, "upto"), (vecs, "vecs")):
                e.dma_start(dst[:, :], io[src]).then_inc(c_ld, 16)

        x_lds = [sem(f"x_loaded_{c}") for c in range(4)]

        cw = sem("conv_weights_scaled")

        def start_dve(e):
            for credit in (acc_rd, ln_x, ln_l):
                e.sem_inc(credit, 2)
            e.memset(lnS, 0.0).then_inc(st_s, 1)
            e.memset(onesm[:, :], 1.0).then_inc(cw, 1)
            split_lo(e, 0, 0)
            for c in range(KC):
                if c % 2 == 0:
                    e.wait_ge(x_lds[c // 2], 16)
                ln_sum(e, 0, c)
            split_lo(e, 1, 1)
            e.wait_ge(c_ld, 16 * 5)
            e.tensor_scalar(vecs[:, 48:240], vecs[:, 48:240], 1.0 / W_SCALE, None, ALU.mult).then_inc(cw, 1)
            ln_dve(e, 0)

        def start_act(e):
            split_hi(e, 0, 0, 0, True)
            for c in range(KC):
                if c % 2 == 0:
                    e.wait_ge(x_lds[c // 2], 16)
                ln_square(e, 0, c)
            split_hi(e, 1, 1, 0, True)
            ln_act(e, 0)

        def start_pool(e):
            e.memset(lnQ, 0.0).then_inc(st_q, 1)
            for c in range(KC):
                ln_square_sum(e, 0, c)
            ln_pool(e, 0)

        def start_pe(e):
            e.wait_ge(c_ld, 16 * 5)
            ln_pe(e, 0)

        QR, QRL = r0h, r0l
        abst = f32(96, 1152)
        wcq = [[f16(101 + 4.5 * s + 1.5 * a, CQ) for a in range(2)] for s in range(2)]
        wqr = [f16(104 + 4.5 * s, CJ * P).rearrange("p (j a r) -> p j a r", j=CJ, a=2) for s in range(2)]
        rcos = f32(110, CJ * S).rearrange("p (j s) -> p j s", j=CJ)
        rsin = f32(112, CJ * S).rearrange("p (j s) -> p j s", j=CJ)
        qhl = [[f16((114, 182)[s] + 2 * k, TOK) for k in range(2)] for s in range(2)]
        rt = [[f32((118, 134, 166)[p] + 4 * k, TOK) for k in range(4)] for p in range(3)]
        ab_ld = sem("query_weights_loaded")
        rope_ld = sem("rotary_tables_loaded")
        wc_hi = sem("wide_query_weights_hi")
        wc_lo = sem("wide_query_weights_split")
        wr_hi = sem("q_r_weights_hi")
        wr_lo = sem("q_r_weights_split")
        q_hi = sem("query_hi")
        q_lo = sem("query_split")
        xc_mm = sem("wide_query_chunk")
        xc_rd = sem("wide_query_rotated")
        y_sum = sem("rotary_sum")
        y_hi = sem("rotary_hi")
        y_lo = [sem("rotary_split_0"), sem("rotary_split_1")]
        y_used = sem("rotary_used")
        qr_hi = sem("q_r_hi")
        qr_lo = sem("q_r_split")
        yh = [[f16(150 + 8 * s + 4 * k, TOK) for k in range(2)] for s in range(2)]
        yl = [[f16(152 + 8 * s + 4 * k, TOK) for k in range(2)] for s in range(2)]

        def load_ab(e, h):
            e.dma_start(abst, one(io["abstream"][bass.ds(h, 1)].rearrange("a p n -> p a n"))).then_inc(ab_ld, 16)

        def xa_sp(e):
            e.wait_ge(ln_l, ln_done(0))
            e.dma_start(rcos, io["rcos"]).then_inc(rope_ld, 16)
            e.dma_start(rsin, io["rsin"]).then_inc(rope_ld, 16)
            load_ab(e, 0)

            def step(h, s):
                e.wait_ge(w_rdy, h)
                load_w(e, h + 1, s)
                e.wait_ge(wr_lo, h)
                load_ab(e, h)
            with e.Fori(0, 7) as i:
                step(i * 2 + 1, 0)
                step(i * 2 + 2, 1)
            step(15, 0)
            e.wait_ge(w_rdy, 16)
            load_w(e, 17, 1)

        def qr_pe(e, h, hs, p):
            P3, s = h * 3 + p, (hs + p) % 2
            if p == 0:
                if not (isinstance(h, int) and h == 0):
                    e.wait_ge(qr_lo, h)
                e.wait_ge(wr_lo, h + 1)
            for part in range(2):
                e.wait_ge(y_lo[part], P3 + 1)
            for k in range(2):
                w = wqr[hs][:, p + 3 * k, :, :].rearrange("p a r -> p (a r)")
                for a, y in enumerate((yh[s][k], yl[s][k])):
                    for c in range(2):
                        mm = e.matmul(bank(6 + c), w, y[:, c * HALF:(c + 1) * HALF], start=(p == 0 and k == 0 and a == 0),
                                      stop=(p == 2 and k == 1 and a == 1))
            mm.then_inc(y_used, 1)

        KSL = [(0, 3), (3, 6), (6, 8)]

        def heads(e, head):
            for h in (0, 1):
                head(h, h, 0)
            with e.Fori(1, 7) as i:
                for hs in range(2):
                    head(i * 2 + hs, hs, i)
            for h in (14, 15):
                head(h, h - 14, 7)

        def xa_pe(e):
            def gemm(h, s, k0, k1):
                if k0 == 0:
                    e.wait_ge(w_rdy, h + 1)
                unit_mm(e, s, bank(0, 2), xnh, xnl, 0, list(range(k0, k1)), k0 == 0, k1 == 8, k1 == 8)

            def head(h, hs, i):
                first, last = isinstance(h, int) and h == 0, isinstance(h, int) and h == 15
                for p in range(3):
                    P3 = h * 3 + p
                    if p == 0:
                        e.wait_ge(q_lo, h + 1)
                        e.wait_ge(wc_lo, h + 1)
                    if p == 2 and not last:
                        gemm(h + 1, 1 - hs, *KSL[p])
                    for k in range(2):
                        if not (first and p == 0):
                            e.wait_ge(xc_rd, P3 * 2 + (k - 1))
                        j = p + 3 * k
                        wh, wl = (wcq[hs][a][:, j * P:(j + 1) * P] for a in range(2))
                        for a, (w, x) in enumerate(((wh, qhl[hs][0]), (wh, qhl[hs][1]), (wl, qhl[hs][0]))):
                            for c in range(2):
                                mm = e.matmul(bank(2 + 2 * k + c), w, x[:, c * HALF:(c + 1) * HALF],
                                              start=(a == 0), stop=(a == 2))
                        mm.then_inc(xc_mm, 1)
                    if p < 2 and not last:
                        gemm(h + 1, 1 - hs, *KSL[p])
                    if not first:
                        qr_pe(e, h - 1, 1 - hs, p)
            e.wait_ge(ln_l, ln_done(0))
            gemm(0, 0, 0, 8)
            heads(e, head)
            for p in range(3):
                qr_pe(e, 15, 1, p)

        def xa_order(e, wide, narrow, q, weights, rotate, y, qr):
            def head(h, hs, i):
                early = isinstance(h, int) and h < 2
                first, last = isinstance(h, int) and h == 0, isinstance(h, int) and h == 15
                for p in range(3):
                    P3, s = h * 3 + p, (hs + p) % 2
                    if p == 0 and not early:
                        qr(h - 2)
                    if p < 2:
                        rotate(p, P3, first)
                    if not (first and p < 2):
                        y(P3 - 2, s, (p + 1) % 3, early and P3 < 4)
                    if p == 0:
                        narrow(h, hs)
                    if p == 1:
                        weights(h, hs, i)
                        if not last:
                            wide(h + 1, 1 - hs)
                    if p == 2:
                        if not last:
                            q(h + 1, 1 - hs)
                        rotate(p, P3, first)
            wide(0, 0)
            q(0, 0)
            heads(e, head)
            y(46, 0, 1, False)
            qr(14)
            y(47, 1, 2, False)
            qr(15)

        def xa_act(e):
            def wide(h, hs):
                e.wait_ge(ab_ld, h * 16 + 16)
                e.activation(wcq[hs][0], abst[:, 0:CQ], ACT.Copy, scale=W_SCALE).then_inc(wc_hi, 1)

            def narrow(h, hs):
                e.activation(wqr[hs][:, :, 0, :], abst[:, CQ:].rearrange("p (j r) -> p j r", j=CJ), ACT.Copy,
                             scale=W_SCALE).then_inc(wr_hi, 1)

            def q(h, hs):
                e.wait_ge(w_used, h + 1)
                e.activation(qhl[hs][0], bank(0, 2), ACT.Copy, scale=1.0 / W_SCALE).then_inc(q_hi, 1)

            def weights(h, s, i):
                split_hi(e, h + 2, s, i + 1)

            def y(P3, s, p, first):
                e.wait_ge(y_sum, P3 * 2 + 2)
                if not first:
                    e.wait_ge(y_used, P3 - 1)
                for k in range(2):
                    e.activation(yh[s][k], rt[p][2 * k], ACT.Copy).then_inc(y_hi, 1)

            def qr(h):
                e.wait_ge(y_used, h * 3 + 3)
                e.activation(one(QR[:, bass.ds(h, 1), :]), bank(6, 2), ACT.Copy,
                             scale=QR_SCALE / W_SCALE).then_inc(qr_hi, 1)
            xa_order(e, wide, narrow, q, weights, lambda *a: None, y, qr)

        def xa_dve(e):
            def wide(h, hs):
                e.wait_ge(wc_hi, h + 1)
                e.scalar_tensor_tensor(out=wcq[hs][1], in0=abst[:, 0:CQ], scalar=W_SCALE, in1=wcq[hs][0],
                                       op0=ALU.mult, op1=ALU.subtract).then_inc(wc_lo, 1)

            def narrow(h, hs):
                e.wait_ge(wr_hi, h + 1)
                e.scalar_tensor_tensor(out=wqr[hs][:, :, 1, :], in0=abst[:, CQ:].rearrange("p (j r) -> p j r", j=CJ),
                                       scalar=W_SCALE, in1=wqr[hs][:, :, 0, :],
                                       op0=ALU.mult, op1=ALU.subtract).then_inc(wr_lo, 1)

            def q(h, hs):
                e.wait_ge(q_hi, h + 1)
                e.scalar_tensor_tensor(out=qhl[hs][1], in0=bank(0, 2), scalar=1.0 / W_SCALE, in1=qhl[hs][0],
                                       op0=ALU.mult, op1=ALU.subtract).then_inc(q_lo, 1)

            def weights(h, s, i):
                split_lo(e, h + 2, s)

            def rotate(p, P3, first):
                if not first:
                    for part in range(2):
                        e.wait_ge(y_lo[part], P3 - 2)
                for k in range(2):
                    j, other = p + 3 * k, p + 3 * (1 - k)
                    e.wait_ge(xc_mm, P3 * 2 + (k + 1))
                    x = bank(2 + 2 * k, 2).rearrange("p (b s) -> p b s", s=S)
                    for dst, table in ((rt[p][2 * k], rcos[:, j, :]), (rt[p][2 * k + 1], rsin[:, other, :])):
                        ins = e.tensor_tensor(dst.rearrange("p (b s) -> p b s", s=S), x, bc(table, NB), ALU.mult)
                    ins.then_inc(xc_rd, 1)

            def y(P3, s, p, first):
                e.wait_ge(y_hi, P3 * 2 + 1)
                e.tensor_tensor(yl[s][0], rt[p][0], yh[s][0], ALU.subtract).then_inc(y_lo[0], 1)

            def qr(h):
                e.wait_ge(qr_hi, h + 1)
                e.scalar_tensor_tensor(out=one(QRL[:, bass.ds(h, 1), :]), in0=bank(6, 2), scalar=QR_SCALE / W_SCALE,
                                       in1=one(QR[:, bass.ds(h, 1), :]), op0=ALU.mult, op1=ALU.subtract).then_inc(qr_lo, 1)
            e.wait_ge(rope_ld, 32)
            xa_order(e, wide, narrow, q, weights, rotate, y, qr)

        def xa_pool(e):
            def low(P3, s, p):
                e.wait_ge(y_hi, P3 * 2 + 2)
                e.tensor_tensor(yl[s][1], rt[p][2], yh[s][1], ALU.subtract).then_inc(y_lo[1], 1)

            def head(h, hs, i):
                for p in range(3):
                    P3, s = h * 3 + p, (hs + p) % 2
                    if not (isinstance(h, int) and P3 < 2):
                        low(P3 - 2, s, (p + 1) % 3)
                    e.wait_ge(xc_rd, P3 * 2 + 2)
                    for k in range(2):
                        e.tensor_tensor(rt[p][2 * k], rt[p][2 * k], rt[p][3 - 2 * k], ALU.add).then_inc(y_sum, 1)
            heads(e, head)
            low(46, 0, 1)
            low(47, 1, 2)

        wkst = f32(64, 2 * H * DC).rearrange("p (a n) -> p a n", a=2)
        wk = [[f16(96 + 16 * a + 8 * k, H * DC).rearrange("p (h d) -> p h d", d=DC) for k in range(2)] for a in range(2)]
        QA = [[[f16(64 + 8 * s + 4 * d + 2 * k, TOK) for k in range(2)] for d in range(2)] for s in range(2)]
        kvst = [f32(80, TOK), f32(84, TOK)]
        km1, km2 = f32(88, TOK), f32(92, TOK)
        kcos, ksin = [f32(128, TOK), f32(136, TOK)], [f32(132, TOK), f32(140, TOK)]
        KV = [[[f16(144 + 8 * s + 4 * l + 2 * k, TOK) for k in range(2)] for l in range(2)] for s in range(2)]
        CC = [[f16(160 + 2 * d + k, HALF) for k in range(2)] for d in range(2)]
        ex_t = [f32(164 + 2 * s, L) for s in range(2)]
        AT = [[f16(168 + 8 * s + 4 * k, 4 * L).rearrange("p (c n) -> p c n", c=4) for k in range(2)] for s in range(2)]
        nmax, rsum, rinv = small[:, 0:2], small[:, 2:4], small[:, 4:6]
        wk_ld = sem("key_value_weights_loaded")
        wk_hi = sem("key_value_weights_hi")
        wk_lo = sem("key_value_weights_split")
        kt_ld = sem("key_tables_loaded")
        kv_ld = [sem("context_loaded"), sem("context_rows_loaded")]
        kv_mul = sem("context_rotated")
        kv_sum = sem("context_rotary_sum")
        kv_hi = sem("context_hi")
        kv_lo = sem("context_split")
        qa_mm = sem("q_a_ready")
        qa_hi = sem("q_a_hi")
        qa_lo = sem("q_a_split")
        sc_mm = sem("scores_ready")
        mx = sem("scores_maximum")
        exd = sem("scores_exp")
        rcp = sem("weights_sum_inverse")
        nrm = sem("attention_normalised")
        tr_mm = sem("attention_transposed")
        at_hi = sem("attention_hi")
        at_lo = sem("attention_split")
        cc_mm = sem("mean_context_ready")
        cc_hi = sem("mean_context_hi")
        cc_lo = sem("mean_context_split")
        cl_mm = sem("values_ready")
        cl_hi = sem("values_hi")
        cl_lo = sem("values_split")

        def xb_sp(e):
            e.wait_ge(w_used, 16)
            for a in range(2):
                e.dma_start(wkst[:, a, :], io["wk"][a]).then_inc(wk_ld, 16)
            e.wait_ge(qr_lo, 16)
            for l in range(2):
                e.dma_start(kcos[l], io["kcos"][l]).then_inc(kt_ld, 16)
                e.dma_start(ksin[l], io["ksin"][l]).then_inc(kt_ld, 16)
            e.wait_ge(wk_lo, 2)
            for l in range(2):
                e.dma_start(kvst[l], io["ctx"][l, 0]).then_inc(kv_ld[l], 16)
            with e.Fori(1, NB) as b:
                for l in range(2):
                    e.wait_ge(kv_mul, b * 2 + (l - 1))
                    e.dma_start(kvst[l], one(io["ctx"][l, bass.ds(b, 1)].rearrange("a p n -> p a n"))).then_inc(kv_ld[l], 16)

        def xb_pe(e):
            def qa(b, s, q, early=False):
                d, half = q // 2, q % 2
                if early == "start":
                    if d:
                        e.wait_ge(qa_lo, half + 1)
                elif q in (0, 3) and not early:
                    e.wait_ge(cl_lo, b * 2 - (3 - d))
                else:
                    e.wait_ge(qa_lo, b * 4 + (q - 1))
                for h in range(8):
                    for a, (w, x) in enumerate(((0, QR), (0, QRL), (1, QR))):
                        mm = e.matmul(bank(6 + half)[:, h * S:(h + 1) * S],
                                      wk[0][w][:, half * 8 + h, d * P:(d + 1) * P],
                                      x[:, half * 8 + h, bass.ds(b * S, S)], start=(a == 0), stop=(a == 2))
                mm.then_inc(qa_mm, 1)

            def scores(b, s, r, start):
                if r == 0:
                    e.wait_ge(kv_lo, b * 2 + 1)
                if r % 4 == 0:
                    e.wait_ge(qa_lo, b * 4 + (3 + r // 4))
                if not (start and r < 2):
                    e.wait_ge(exd, b * 8 + (r - 1))
                n = 0
                for d in range(2):
                    for w, x in ((0, 0), (0, 1), (1, 0)):
                        mm = e.matmul(bank(2 + r % 2), QA[s][d][w][:, r * P:(r + 1) * P],
                                      KV[s][0][x][:, d * L:(d + 1) * L], start=(n == 0), stop=(n == 5))
                        n += 1
                mm.then_inc(sc_mm, 1)

            def trans(tile, par, early):
                e.wait_ge(nrm, tile + 1)
                if not early:
                    e.wait_ge(at_lo, tile - 1)
                for c in range(4):
                    mm = e.transpose(bank(4 + par)[:, c * P:(c + 1) * P], ex_t[par][:, c * P:(c + 1) * P], xid[:, :])
                mm.then_inc(tr_mm, 1)

            def cc(G, g, s, d, early):
                if not early:
                    e.wait_ge(cc_lo, G * 2 + (d - 1))
                e.wait_ge(at_lo, G * 4 + 4)
                e.wait_ge(kv_lo, (G - g) + 2)
                n = 0
                for c in range(4):
                    for w, x in ((0, 0), (0, 1), (1, 0)):
                        mm = e.matmul(bank(d), KV[s][1][w][:, c * DC + d * P:c * DC + (d + 1) * P], AT[g][x][:, c, :],
                                      start=(n == 0), stop=(n == 11))
                        n += 1
                mm.then_inc(cc_mm, 1)

            def cl(G, g, last):
                e.wait_ge(cc_lo, G * 2 + 2)
                if g == 0:
                    e.wait_ge(qa_lo, 64 if last else G * 2 + 7)
                    if last:
                        e.wait_ge(cl_lo, G - 1)
                elif last:
                    e.wait_ge(cl_lo, G - 1)
                else:
                    e.wait_ge(qa_lo, G * 2 + 8)
                for h in range(8):
                    n = 0
                    for d in range(2):
                        for w, x in ((0, 0), (0, 1), (1, 0)):
                            mm = e.matmul(bank(6 + g)[:, h * S:(h + 1) * S], wk[1][w][:, 8 * g + h, d * P:(d + 1) * P],
                                          CC[d][x][:, h * S:(h + 1) * S], start=(n == 0), stop=(n == 5))
                            n += 1
                mm.then_inc(cl_mm, 1)

            def batch(b, s, first=False, last=False):
                for r in range(8):
                    if r == 3 and not last:
                        qa(b + 1, 1 - s, 0, first)
                    scores(b, s, r, first)
                    if r in (0, 4) and not first:
                        cl(b * 2 - 2 + r // 4, r // 4, last and r == 4)
                    if r in (1, 2) and not first:
                        cc(b * 2 - 1, 1, 1 - s, r - 1, False)
                    if r in (3, 4, 7) and not last:
                        qa(b + 1, 1 - s, {3: 1, 4: 2, 7: 3}[r], first)
                    if r in (5, 6):
                        cc(b * 2, 0, s, r - 5, first)
                    if not (first and r == 0):
                        trans(b * 8 + (r - 1), (r - 1) % 2, first and r < 3)
            e.wait_ge(wk_lo, 2)
            e.wait_ge(qr_lo, 16)
            for q in range(4):
                qa(0, 0, q, "start")
            batch(0, 0, first=True)
            with e.Fori(0, 7) as i:
                batch(i * 2 + 1, 1)
                batch(i * 2 + 2, 0)
            batch(15, 1, last=True)
            trans(127, 1, False)
            cl(30, 0, True)
            cc(31, 1, 1, 0, False)
            cc(31, 1, 1, 1, False)
            cl(31, 1, True)

        def xb_order(e, exp_, norm, attn, mean, vals, qa, kmul, khi, klo):
            def batch(b, s, first=False, last=False):
                for r in range(8):
                    if not (first and r < 2):
                        q = (r - 2) % 8
                        attn(b * 8 + (r - 2), q % 2, q // 4, q % 4)
                    if r in (1, 5) and not first:
                        vals(b * 2 - 2 + r // 4, r // 4, b - 1)
                    if r in (2, 3) and not first:
                        mean(b * 2 - 1, r - 2)
                    if r in (6, 7):
                        mean(b * 2, r - 6)
                    if r == 3 and not last:
                        qa(b + 1, 1 - s, 0)
                    if r == 5 and not last:
                        qa(b + 1, 1 - s, 2)
                    if r == 0:
                        khi(b, s, 1)
                    if r == 4 and not last:
                        khi(b + 1, 1 - s, 0)
                    exp_(b * 8 + r, r % 2, first and r < 2)
                    if r in (1, 2, 5, 6) and not last:
                        kmul(b + 1, r // 5, (r - 1) % 4)
                    if r == 0:
                        klo(b, s, 1)
                    if r == 4 and not last:
                        klo(b + 1, 1 - s, 0)
                    norm(b * 8 + r, r % 2)
                    if r in (3, 7) and not last:
                        qa(b + 1, 1 - s, r // 7 * 2 + 1)
            for l in range(2):
                for part in range(2):
                    kmul(0, l, part)
                if l == 0:
                    khi(0, 0, 0)
                    klo(0, 0, 0)
            for q in range(4):
                qa(0, 0, q)
            batch(0, 0, first=True)
            with e.Fori(0, 7) as i:
                batch(i * 2 + 1, 1)
                batch(i * 2 + 2, 0)
            batch(15, 1, last=True)
            attn(126, 0, 1, 2)
            attn(127, 1, 1, 3)
            vals(30, 0, 15)
            mean(31, 0)
            mean(31, 1)
            vals(31, 1, 15)

        def batch_cols(t, g, b):
            return t[:, 8 * g:8 * g + 8, bass.ds(b * S, S)]

        def xb_act(e):
            def exp_(tile, par, early):
                e.wait_ge(mx, tile + 1)
                if not early:
                    e.wait_ge(tr_mm, tile - 1)
                e.activation(ex_t[par], bank(2 + par), ACT.Exp, bias=nmax[:, par:par + 1],
                             accum_out=rsum[:, par:par + 1]).then_inc(exd, 1)

            def attn(tile, par, g, q):
                e.wait_ge(tr_mm, tile + 1)
                e.activation(AT[g][0][:, :, q * P:(q + 1) * P], bank(4 + par).rearrange("p (c n) -> p c n", c=4),
                             ACT.Copy).then_inc(at_hi, 1)

            def mean(G, d):
                e.wait_ge(cc_mm, G * 2 + (d + 1))
                e.activation(CC[d][0], bank(d), ACT.Copy, scale=1.0 / PR_SCALE).then_inc(cc_hi, 1)

            def vals(G, g, b):
                e.wait_ge(cl_mm, G + 1)
                e.activation(batch_cols(QR, g, b), bank(6 + g).rearrange("p (h s) -> p h s", s=S), ACT.Copy,
                             scale=1.0 / W_SCALE).then_inc(cl_hi, 1)

            def qa(b, s, q):
                d, half = q // 2, q % 2
                e.wait_ge(qa_mm, b * 4 + (q + 1))
                e.activation(QA[s][d][0][:, half * HALF:(half + 1) * HALF], bank(6 + half), ACT.Copy,
                             scale=1.0 / (W_SCALE * QR_SCALE)).then_inc(qa_hi, 1)

            def khi(b, s, l):
                e.wait_ge(kv_sum, b * 2 + (l + 1))
                e.activation(KV[s][l][0], km1, ACT.Copy).then_inc(kv_hi, 1)
            none = lambda *a: None
            e.wait_ge(qr_lo, 16)
            e.wait_ge(wk_ld, 32)
            for a in range(2):
                e.activation(wk[a][0], wkst[:, a, :].rearrange("p (h d) -> p h d", d=DC), ACT.Copy,
                             scale=W_SCALE).then_inc(wk_hi, 1)
            xb_order(e, exp_, none, attn, mean, vals, qa, none, khi, none)

        def xb_dve(e):
            def exp_(tile, par, early):
                e.wait_ge(sc_mm, tile + 1)
                e.tensor_reduce(nmax[:, par:par + 1], bank(2 + par), AXX, ALU.max, negate=True).then_inc(mx, 1)

            def norm(tile, par):
                e.wait_ge(exd, tile + 1)
                e.reciprocal(rinv[:, par:par + 1], rsum[:, par:par + 1]).then_inc(rcp, 1)
                e.wait_ge(rcp, tile + 1)
                e.tensor_scalar(ex_t[par], ex_t[par], rinv[:, par:par + 1], PR_SCALE, ALU.mult, ALU.mult).then_inc(nrm, 1)

            def attn(tile, par, g, q):
                e.wait_ge(at_hi, tile + 1)
                a, src = AT[g], bank(4 + par).rearrange("p (c n) -> p c n", c=4)
                e.tensor_tensor(a[1][:, :, q * P:(q + 1) * P], src, a[0][:, :, q * P:(q + 1) * P],
                                ALU.subtract).then_inc(at_lo, 1)

            def mean(G, d):
                e.wait_ge(cc_hi, G * 2 + (d + 1))
                e.scalar_tensor_tensor(out=CC[d][1], in0=bank(d), scalar=1.0 / PR_SCALE, in1=CC[d][0],
                                       op0=ALU.mult, op1=ALU.subtract).then_inc(cc_lo, 1)

            def vals(G, g, b):
                e.wait_ge(cl_hi, G + 1)
                e.scalar_tensor_tensor(out=batch_cols(QRL, g, b), in0=bank(6 + g).rearrange("p (h s) -> p h s", s=S),
                                       scalar=1.0 / W_SCALE, in1=batch_cols(QR, g, b),
                                       op0=ALU.mult, op1=ALU.subtract).then_inc(cl_lo, 1)

            def qa(b, s, q):
                d, half = q // 2, q % 2
                e.wait_ge(qa_hi, b * 4 + (q + 1))
                c = slice(half * HALF, (half + 1) * HALF)
                e.scalar_tensor_tensor(out=QA[s][d][1][:, c], in0=bank(6 + half), scalar=1.0 / (W_SCALE * QR_SCALE),
                                       in1=QA[s][d][0][:, c], op0=ALU.mult, op1=ALU.subtract).then_inc(qa_lo, 1)

            def kmul(b, l, part):
                if part == 0:
                    e.wait_ge(kv_ld[l], b * 16 + 16)
                    if not (isinstance(b, int) and b == 0 and l == 0):
                        e.wait_ge(kv_lo, b * 2 + l)
                    e.tensor_tensor(km1, kvst[l], kcos[l], ALU.mult)
                    return
                sh = (lambda t: t.rearrange("p (c a n) -> p c a n", a=2, n=(L, P)[l]))
                for a in range(2):
                    ins = e.tensor_tensor(sh(km2)[:, :, a, :], sh(kvst[l])[:, :, 1 - a, :], sh(ksin[l])[:, :, a, :], ALU.mult)
                ins.then_inc(kv_mul, 1)

            def klo(b, s, l):
                e.wait_ge(kv_hi, b * 2 + (l + 1))
                e.tensor_tensor(KV[s][l][1], km1, KV[s][l][0], ALU.subtract).then_inc(kv_lo, 1)
            e.wait_ge(kt_ld, 64)
            for a in range(2):
                e.wait_ge(wk_hi, a + 1)
                e.scalar_tensor_tensor(out=wk[a][1].rearrange("p h d -> p (h d)"), in0=wkst[:, a, :], scalar=W_SCALE,
                                       in1=wk[a][0].rearrange("p h d -> p (h d)"),
                                       op0=ALU.mult, op1=ALU.subtract).then_inc(wk_lo, 1)
            xb_order(e, exp_, norm, attn, mean, vals, qa, kmul, lambda *a: None, klo)

        def xb_pool(e):
            with e.Fori(0, 2 * NB) as k:
                e.wait_ge(kv_mul, k + 1)
                e.tensor_tensor(km1, km1, km2, ALU.add).then_inc(kv_sum, 1)

        def residual_pe(e, name, sh, sl):
            pairs(e, KC, lambda m, par, i, last: gemm_pe(e, name, m, par, sh, sl))

        def residual_act(e, name, z):
            def chunk(m, par, i, last):
                split_next(e, "hi", name, m, par, i)
                ln_square(e, z, m)
            pairs(e, KC, chunk)
            ln_act(e, z)

        def residual_dve(e, name, z):
            def chunk(m, par, i, last):
                split_next(e, "lo", name, m, par, i)
                e.wait_ge(w_used, used(name, m))
                e.scalar_tensor_tensor(out=x_chunk(m), in0=bank(2 * par, 2), scalar=1.0 / W_SCALE, in1=x_chunk(m),
                                       op0=ALU.mult, op1=ALU.add).then_inc(acc_rd, 1)
            pairs(e, KC, chunk)
            ln_dve(e, z)

        def residual_pool(e, name, z):
            e.memset(lnS, 0.0).then_inc(st_s, 1)
            e.memset(lnQ, 0.0).then_inc(st_q, 1)

            def chunk(m, par, i, last):
                ln_sum(e, z, m)
                ln_square_sum(e, z, m)
            pairs(e, KC, chunk)
            ln_pool(e, z)

        def xo_sp(e):
            e.wait_ge(cl_lo, 32)
            e.dma_start(XT, io["xT"]).then_inc(xr_ld, 16)
        xr_ld = sem("x_reloaded")

        KH, KL = r0h, r0l
        yc = f32(96, TOK)
        sv = [f32(100 + 4 * s, TOK) for s in range(2)]
        gm = f32(108, TOK)
        qdh, qdl = f16(112, TOK), f16(114, TOK)
        qsq = f32(116, TOK)
        sA = f32(120, 2048).rearrange("p (h i j) -> p h i j", h=8, i=T)
        sT = f32(128, 2048).rearrange("p (h i j) -> p h i j", h=8, i=T)
        sU = f32(136, 2048).rearrange("p (h i j) -> p h i j", h=8, i=T)
        lower = f32(144, 256).rearrange("p (i j) -> p i j", i=T)
        eye = f32(145, 256).rearrange("p (i j) -> p i j", i=T)
        gc = [f32(146 + s / 2, P).rearrange("p (g j) -> p g j", g=G8) for s in range(2)]
        betaq = f32(147, P).rearrange("p (h t) -> p h t", h=8)
        rk = f32(147.5, P).rearrange("p (h t) -> p h t", h=8)
        rkb = f32(148, P).rearrange("p (h t) -> p h t", h=8)
        nhalf = f32(148.5, P).rearrange("p (h t) -> p h t", h=8)
        q2e = f32(149, P)
        beta = f32(149.5, TOK)[0:H, :]
        wbh, wbl = f16(116, P), f16(116.25, P)
        wbst = f32(117, P)
        d_ld = sem("delta_constants_loaded")
        wb_hi = sem("beta_weights_hi")
        wb_lo = sem("beta_weights_split")
        b_mm = sem("beta_ready")
        b_sg = sem("beta_sigmoid")
        b_st = sem("beta_stored")
        seq_ld = sem("sequences_loaded")
        cv = sem("conv_first_taps")
        cy = sem("conv_last_tap_input")
        si = sem("silu")
        k_hi = sem("key_hi")
        k_lo = sem("key_split")
        g_mm = sem("gram_ready")
        g_ms = sem("gram_masked")
        g_c = sem("gram_compact")
        g_st = [sem("gram_stored_0"), sem("gram_stored_1")]
        pr = sem("solve_prepared")
        sl_u = sem("solve_product")
        sl_t = sem("solve_row")
        tc_st = sem("inverse_stored")
        q_h2 = sem("delta_query_hi")
        q_sq = sem("delta_query_square")
        q_l2 = sem("delta_query_split")
        p_mm = sem("products_ready")
        p_ms = sem("products_masked")
        p_hi = sem("products_hi")
        p_lo = sem("products_split")
        q2_rd = sem("query_norms")
        BASE = {"dk": 0, "dq": 16, "dv": 32}

        def conv_act(e, name, m, par, between=None):
            e.wait_ge(w_used, used(name, m))
            if not (isinstance(m, int) and m == 0 and name == "dk"):
                e.wait_ge(si, m + BASE[name])
            e.activation(yc, bank(2 * par, 2), ACT.Copy, scale=convw[name][:, bass.ds(m * 4 + 3, 1)]).then_inc(cy, 1)
            if between:
                between()
            e.wait_ge(acc_rd, acc_done(name, m))
            e.activation(sv[par].rearrange("p (b t) -> p t b", t=T), yc.rearrange("p (t b) -> p t b", t=T),
                         ACT.Silu).then_inc(si, 1)

        def conv_dve(e, name, m, par):
            e.wait_ge(cy, m + (BASE[name] + 1))
            for back in (1, 2, 3):
                n = TOK - DB * back
                if back > 1:
                    e.wait_ge(cv, m * 2 + (BASE[name] * 2 + back - 1))
                e.scalar_tensor_tensor(out=yc[:, DB * back:], in0=bank(2 * par, 2)[:, 0:n],
                                       scalar=convw[name][:, bass.ds(m * 4 + (3 - back), 1)], in1=yc[:, DB * back:],
                                       op0=ALU.mult, op1=ALU.add).then_inc(acc_rd if back == 3 else cv, 1)

        def blocks(e, dst, w, x, inc):
            for g in range(G8):
                cols = slice(g * P, (g + 1) * P)
                for a, (i, j) in enumerate(((0, 0), (0, 1), (1, 0))):
                    mm = e.matmul(dst[:, cols], w[i][:, cols], x[j][:, cols], start=(a == 0), stop=(a == 2))
            mm.then_inc(inc, 1)

        def chunk_of(t, h):
            return one(t[:, bass.ds(h, 1), :])

        def dk_sp(e):
            e.wait_ge(ln_l, ln_done(1))
            for dst, src in ((lower, "lower"), (eye, "eye"), (wbst, "wb")):
                e.dma_start(dst, io[src]).then_inc(d_ld, 16)

        def beta_pe(e):
            e.wait_ge(wb_lo, 1)
            for k in range(KC):
                for a, (w, x) in enumerate(((wbh, xnh), (wbh, xnl), (wbl, xnh))):
                    for c in range(2):
                        mm = e.matmul(bank(4 + c)[0:H, :], w[:, k * H:(k + 1) * H], x[:, k, c * HALF:(c + 1) * HALF],
                                      start=(k == 0 and a == 0), stop=(k == KC - 1 and a == 2))
            mm.then_inc(b_mm, 1)

        def dk_pe(e):
            e.wait_ge(ln_l, ln_done(1))
            beta_pe(e)

            def gram(h, par):
                e.wait_ge(k_lo, h + 1)
                if isinstance(h, int) and h < 2:
                    e.wait_ge(b_sg, 1)
                else:
                    e.wait_ge(g_ms, h - 1)
                k = (chunk_of(KH, h), chunk_of(KL, h))
                blocks(e, bank(4 + 2 * par, 2), k, k, g_mm)

            def head(h, par, i, last):
                gemm_pe(e, "dk", h, par, xnh, xnl)
                if not (isinstance(h, int) and h == 0):
                    gram(h - 1, 1 - par)
            pairs(e, H, head, peel=2)
            gram(15, 1)

        def dk_act(e):
            e.wait_ge(d_ld, 48)
            e.activation(wbh, wbst, ACT.Copy, scale=W_SCALE).then_inc(wb_hi, 1)
            e.wait_ge(b_mm, 1)
            e.activation(beta, bank(4, 2)[0:H, :], ACT.Sigmoid, scale=1.0 / W_SCALE).then_inc(b_sg, 1)
            e.wait_ge(b_sg, 1)
            e.dma_start(io["beta_s"], beta).then_inc(b_st, 16)

            def store(h, par):
                e.wait_ge(g_c, h + 1)
                e.dma_start(io["gram_s"][bass.ds(h, 1)].rearrange("a g (p j) -> p (a g) j", j=T), gc[par]).then_inc(g_st[par], 16)

            def head(h, par, i, last):
                split_next(e, "hi", "dk", h, par, i)
                conv_act(e, "dk", h, par)
                e.wait_ge(si, h + 1)
                e.activation(chunk_of(KH, h), sv[par], ACT.Copy).then_inc(k_hi, 1)
                if not (isinstance(h, int) and h == 0):
                    store(h - 1, 1 - par)
            pairs(e, H, head, peel=2)
            store(15, 1)

        def dk_dve(e):
            e.wait_ge(wb_hi, 1)
            e.scalar_tensor_tensor(out=wbl, in0=wbst, scalar=W_SCALE, in1=wbh, op0=ALU.mult,
                                   op1=ALU.subtract).then_inc(wb_lo, 1)

            def gram(h, par):
                e.wait_ge(g_mm, h + 1)
                if not (isinstance(h, int) and h < 1):
                    e.wait_ge(g_c, h)
                e.tensor_tensor(gm.rearrange("p (g n) -> p g n", g=G8), bank(4 + 2 * par, 2).rearrange("p (g n) -> p g n", g=G8),
                                bc(same[:, :], G8), ALU.mult).then_inc(g_ms, 1)
                e.wait_ge(g_ms, h + 1)
                if isinstance(h, int):
                    if h >= 2:
                        e.wait_ge(g_st[par], 16 * (h // 2))
                else:
                    e.wait_ge(g_st[par], stored[0])
                e.tensor_reduce(gc[par], gm.rearrange("p (g b j) -> p g j b", g=G8, b=8), AXX, ALU.add).then_inc(g_c, 1)
            stored = [None]

            def head(h, par, i, last):
                split_next(e, "lo", "dk", h, par, i)
                conv_dve(e, "dk", h, par)
                if not (isinstance(h, int) and h == 0):
                    stored[0] = (i - (1 - par)) * 16
                    gram(h - 1, 1 - par)
                e.wait_ge(k_hi, h + 1)
                e.tensor_tensor(chunk_of(KL, h), sv[par], chunk_of(KH, h), ALU.subtract).then_inc(k_lo, 1)
            pairs(e, H, head, peel=2)
            gram(15, 1)

        def solve_pool(e):
            e.wait_ge(d_ld, 48)
            e.wait_ge(b_st, 16)
            for par in range(2):
                e.wait_ge(g_st[par], 128)
            half = lambda t, par: t[64 * par:64 * par + 64]
            for par in range(2):
                e.dma_start(half(sA, par).rearrange("p h i j -> p h (i j)"),
                            io["gram_s"].rearrange("(h a) g (b n) -> a h (g b) n", a=2, b=8)[par].rearrange("h b n -> b h n")).then_inc(seq_ld, 16)
                with nc.allow_non_contiguous_dma(reason="beta by sequence: 64 KiB once"):
                    for h in range(8):
                        e.dma_start(half(betaq, par)[:, h, :],
                                    io["beta_s"].rearrange("(h a) (t b) -> a h b t", a=2, t=T)[par, h]).then_inc(seq_ld, 16)
            e.wait_ge(seq_ld, 16 * 18)
            n = [0]

            def then(ins):
                ins.then_inc(pr, 1)
                n[0] += 1
                e.wait_ge(pr, n[0])
            flat = lambda t: t.rearrange("p h i j -> p h (i j)")
            then(e.memset(nhalf, -0.5))
            then(e.tensor_scalar(rk, flat(sA)[:, :, 0:256:17], 1e-12, None, ALU.add))
            then(e.tensor_tensor(rk, rk, nhalf, ALU.pow))
            then(e.tensor_tensor(rkb, rk, betaq, ALU.mult))
            then(e.tensor_tensor(sA, sA, bc(rkb, T, 3), ALU.mult))
            then(e.tensor_tensor(sA, sA, bc(rk, T, 2), ALU.mult))
            then(e.tensor_tensor(flat(sA), flat(sA), bc(lower.rearrange("p i j -> p (i j)"), 8), ALU.mult))
            e.tensor_copy(flat(sT), bc(eye.rearrange("p i j -> p (i j)"), 8)).then_inc(sl_t, 1)
            with e.Fori(0, T - 1) as j:
                e.wait_ge(sl_t, j + 1)
                e.tensor_tensor(sU, sA[:, :, :, bass.ds(j, 1)].to_broadcast([P, 8, T, T]),
                                sT[:, :, bass.ds(j, 1), :].to_broadcast([P, 8, T, T]), ALU.mult).then_inc(sl_u, 1)
                e.wait_ge(sl_u, j + 1)
                e.tensor_tensor(flat(sT), flat(sT), flat(sU), ALU.subtract).then_inc(sl_t, 1)
            e.wait_ge(sl_t, T)
            then(e.tensor_tensor(sT, sT, bc(rk, T, 3), ALU.mult))
            then(e.tensor_tensor(sT, sT, bc(betaq, T, 2), ALU.mult))
            for par in range(2):
                e.dma_start(io["inv_s"].rearrange("(h a) g (b n) -> a h (g b) n", a=2, b=8)[par].rearrange("h b n -> b h n"),
                            half(sT, par).rearrange("p h i j -> p h (i j)")).then_inc(tc_st, 16)

        def dq_pe(e):
            def prod(h, par):
                e.wait_ge(q_l2, h + 1)
                e.wait_ge(q_sq, h + 1)
                if isinstance(h, int) and h == 0:
                    e.wait_ge(g_ms, 16)
                else:
                    e.wait_ge(p_ms, h)
                blocks(e, bank(4, 2), (chunk_of(KH, h), chunk_of(KL, h)), (qdh, qdl), p_mm0)
                for g in range(G8):
                    mm = e.matmul(bank(6)[:, bass.ds(h * G8 + g, 1)] if not isinstance(h, int) else bank(6)[:, h * G8 + g:h * G8 + g + 1],
                                  qsq[:, g * P:(g + 1) * P], onesm[:, :], start=True, stop=True)
                mm.then_inc(p_mm, 1)

            def head(h, par, i, last):
                gemm_pe(e, "dq", h, par, xnh, xnl)
                if not (isinstance(h, int) and h == 0):
                    prod(h - 1, 1 - par)
            pairs(e, H, head, peel=1)
            prod(15, 1)
        p_mm0 = sem("products_alone_ready")

        def dq_act(e):
            def part(h):
                e.wait_ge(p_ms, h + 1)
                e.activation(chunk_of(KH, h), gm, ACT.Copy).then_inc(p_hi, 1)

            def head(h, par, i, last):
                split_next(e, "hi", "dq", h, par, i)
                conv_act(e, "dq", h, par)
                e.wait_ge(si, h + 17)
                if not (isinstance(h, int) and h == 0):
                    e.wait_ge(p_mm, h)
                e.activation(qdh, sv[par], ACT.Copy).then_inc(q_h2, 1)
                e.activation(qsq, sv[par], ACT.Square).then_inc(q_sq, 1)
                if not (isinstance(h, int) and h == 0):
                    part(h - 1)
            pairs(e, H, head, peel=1)
            part(15)

        def dq_dve(e):
            def mask(h):
                e.wait_ge(p_mm, h + 1)
                if isinstance(h, int) and h == 0:
                    e.wait_ge(g_c, 16)
                else:
                    e.wait_ge(p_lo, h)
                e.tensor_tensor(gm.rearrange("p (g n) -> p g n", g=G8), bank(4, 2).rearrange("p (g n) -> p g n", g=G8),
                                bc(upto[:, :], G8), ALU.mult).then_inc(p_ms, 1)

            def low(h):
                e.wait_ge(p_hi, h + 1)
                e.tensor_tensor(chunk_of(KL, h), gm, chunk_of(KH, h), ALU.subtract).then_inc(p_lo, 1)

            def head(h, par, i, last):
                split_next(e, "lo", "dq", h, par, i)
                conv_dve(e, "dq", h, par)
                if not (isinstance(h, int) and h == 0):
                    mask(h - 1)
                e.wait_ge(q_h2, h + 1)
                e.tensor_tensor(qdl, sv[par], qdh, ALU.subtract).then_inc(q_l2, 1)
                if not (isinstance(h, int) and h == 0):
                    low(h - 1)
            pairs(e, H, head, peel=1)
            mask(15)
            low(15)
            e.tensor_scalar(q2e, bank(6)[:, 0:P], LN_EPS * 128, LN_EPS * 128 * 1e-12, ALU.mult, ALU.add).then_inc(q2_rd, 1)

        VT = [f16(108 + 2 * k, TOK) for k in range(2)]
        WT = [f16(112 + 2 * k, TOK) for k in range(2)]
        osq, osc = f32(116, TOK), f32(120, TOK)
        tcs = [f32(124 + s / 2, P).rearrange("p (g j) -> p g j", g=G8) for s in range(2)]
        tcp = [[f16(125 + s / 2 + k / 4, P).rearrange("p (g j) -> p g j", g=G8) for k in range(2)] for s in range(2)]
        TB = [[f16(128 + 4 * s + 2 * k, TOK) for k in range(2)] for s in range(2)]
        same16 = f16(136, P)
        osum, ofac, otmp = small[:, 16:24], small[:, 24:32], small[:, 32:40]
        nh8 = small[:, 40:48]
        tc_ld = [sem("inverse_loaded_0"), sem("inverse_loaded_1")]
        v_c = sem("value_constants")
        tb_c = sem("inverse_parts")
        tb_d = sem("inverse_blocks")
        vt_mm = sem("values_turned")
        vt_hi = sem("values_turned_hi")
        vt_lo = sem("values_turned_split")
        wt_mm = sem("delta_weights_ready")
        wt_hi = sem("delta_weights_hi")
        wt_lo = sem("delta_weights_split")
        o_mm = sem("delta_output_ready")
        o_sq = sem("delta_output_square")
        o_sm = sem("delta_output_square_sum")
        o_ms = sem("delta_output_mean_square")
        o_fc = sem("delta_output_factor")
        o_sc = sem("delta_output_scaled")
        ot_mm = sem("delta_output_turned")
        ot_hi = sem("delta_output_hi")
        ot_lo = sem("delta_output_split")

        def dv_sp(e, u0):
            def tc(h, s):
                e.dma_start(tcs[s], io["inv_s"][bass.ds(h, 1)].rearrange("a g (p j) -> p (a g) j", j=T)).then_inc(tc_ld[s], 16)
            e.wait_ge(tc_st, 32)
            e.wait_ge(q2_rd, 1)
            tc(0, 0)
            tc(1, 1)
            with e.Fori(1, 8) as i:
                for s in range(2):
                    e.wait_ge(w_rdy, i * 2 + (u0 - 2 + s - 1))
                    load_w(e, i * 2 + (u0 - 2 + s), s)
                    e.wait_ge(tb_c, i * 2 + (s - 1))
                    tc(i * 2 + s, s)

        def steps(e, body):
            for h in range(2):
                body(h, h % 2, h // 2)
            with e.Fori(1, 8) as i:
                for par in range(2):
                    body(i * 2 + par, par, i)
            for h in (16, 17):
                body(h, h % 2, h // 2)

        def has(h, back):
            return not isinstance(h, int) or 0 <= h - back < H

        def dv_pe(e):
            def step(h, par, i):
                if has(h, 0):
                    gemm_pe(e, "dv", h, par, xnh, xnl, parts=(0, 3))
                if has(h, 2):
                    e.wait_ge(o_sc, h - 1)
                    if has(h, 1):
                        e.wait_ge(wt_lo, h)
                    for g in range(G8):
                        mm = e.transpose(bank(6, 2)[:, g * P:(g + 1) * P], osc[:, g * P:(g + 1) * P], xid[:, :])
                    mm.then_inc(ot_mm, 1)
                if has(h, 0):
                    gemm_pe(e, "dv", h, par, xnh, xnl, parts=(3, 5))
                if has(h, 1):
                    e.wait_ge(si, h + 32)
                    if has(h, 2):
                        e.wait_ge(o_sc, h - 1)
                    for g in range(G8):
                        mm = e.transpose(bank(4, 2)[:, g * P:(g + 1) * P], sv[1 - par][:, g * P:(g + 1) * P], xid[:, :])
                    mm.then_inc(vt_mm, 1)
                if has(h, 0):
                    gemm_pe(e, "dv", h, par, xnh, xnl, parts=(5, 8))
                if has(h, 1):
                    e.wait_ge(vt_lo, h)
                    e.wait_ge(wt_lo, h)
                    blocks(e, bank(4, 2), WT, VT, o_mm)
                if has(h, 0):
                    e.wait_ge(tb_d, h + 1)
                    if has(h, 2):
                        e.wait_ge(ot_lo, h - 1)
                    blocks(e, bank(6, 2), TB[par], (chunk_of(KH, h), chunk_of(KL, h)), wt_mm)
            e.wait_ge(q2_rd, 1)
            steps(e, step)

        def turned(t):
            return t.rearrange("p (b t) -> p t b", t=T)

        def straight(t):
            return t.rearrange("p (t b) -> p t b", t=T)

        def dv_act(e):
            def step(h, par, i):
                if has(h, 2):
                    e.wait_ge(o_mm, h - 1)
                    e.activation(osq, bank(4, 2), ACT.Square).then_inc(o_sq, 1)
                if has(h, 1):
                    e.wait_ge(wt_mm, h)
                    e.activation(WT[0], bank(6, 2), ACT.Copy).then_inc(wt_hi, 1)
                def turned_output():
                    if has(h, 2):
                        e.wait_ge(ot_mm, h - 1)
                        e.activation(straight(chunk_of(KH, h - 2)), turned(bank(6, 2)), ACT.Copy, scale=gno).then_inc(ot_hi, 1)
                if has(h, 1):
                    conv_act(e, "dv", h - 1, 1 - par, turned_output)
                    e.wait_ge(vt_mm, h)
                    e.activation(VT[0], bank(4, 2), ACT.Copy).then_inc(vt_hi, 1)
                else:
                    turned_output()
                if has(h, 0):
                    split_next(e, "hi", "dv", h, par, i)
            steps(e, step)

        def dv_dve(e):
            def step(h, par, i):
                if has(h, 2):
                    e.wait_ge(o_sq, h - 1)
                    e.tensor_reduce(osum, osq.rearrange("p (g d) -> p g d", g=G8), AXX, ALU.add).then_inc(o_sm, 1)
                    e.wait_ge(o_sm, h - 1)
                    e.scalar_tensor_tensor(out=otmp, in0=osum, scalar=1.0 / P,
                                           in1=q2e[:, bass.ds((h - 2) * G8, G8)] if not isinstance(h, int) else q2e[:, (h - 2) * G8:(h - 1) * G8],
                                           op0=ALU.mult, op1=ALU.add).then_inc(o_ms, 1)
                if has(h, 1):
                    e.wait_ge(wt_hi, h)
                    e.tensor_tensor(WT[1], bank(6, 2), WT[0], ALU.subtract).then_inc(wt_lo, 1)
                if has(h, 2):
                    e.wait_ge(o_fc, h - 1)
                    e.tensor_tensor(osc.rearrange("p (g d) -> p g d", g=G8), bank(4, 2).rearrange("p (g d) -> p g d", g=G8),
                                    bc(ofac, P, 2), ALU.mult).then_inc(o_sc, 1)
                if has(h, 1):
                    conv_dve(e, "dv", h - 1, 1 - par)
                if has(h, 2):
                    e.wait_ge(ot_hi, h - 1)
                    e.scalar_tensor_tensor(out=straight(chunk_of(KL, h - 2)), in0=turned(bank(6, 2)), scalar=gno,
                                           in1=straight(chunk_of(KH, h - 2)), op0=ALU.mult, op1=ALU.subtract).then_inc(ot_lo, 1)
                if has(h, 1):
                    e.wait_ge(vt_hi, h)
                    e.tensor_tensor(VT[1], bank(4, 2), VT[0], ALU.subtract).then_inc(vt_lo, 1)
                if has(h, 0):
                    split_next(e, "lo", "dv", h, par, i)
            steps(e, step)

        def dv_pool(e):
            e.wait_ge(tc_st, 32)
            e.wait_ge(q2_rd, 1)
            e.tensor_copy(same16, same[:, :]).then_inc(v_c, 1)
            e.memset(nh8, -0.5).then_inc(v_c, 1)
            e.wait_ge(v_c, 2)

            def step(h, par, i):
                if has(h, 2):
                    e.wait_ge(o_ms, h - 1)
                    e.tensor_tensor(ofac, otmp, nh8, ALU.pow).then_inc(o_fc, 1)
                if has(h, 0):
                    e.wait_ge(tc_ld[par], (i + 1) * 16)
                    e.tensor_tensor(tcp[par][0], tcs[par], onesm[:, :].unsqueeze(2).to_broadcast([P, G8, T]),
                                    ALU.mult).then_inc(tb_h, 1)
                    e.wait_ge(tb_h, h + 1)
                    e.tensor_tensor(tcp[par][1], tcs[par], tcp[par][0], ALU.subtract).then_inc(tb_c, 1)
                    e.wait_ge(tb_c, h + 1)
                    if has(h, 2):
                        e.wait_ge(wt_mm, h - 1)
                    for k in range(2):
                        ins = e.tensor_tensor(TB[par][k].rearrange("p (g b j) -> p g b j", g=G8, b=8),
                                              bc(tcp[par][k], 8, 2),
                                              bc(same16.rearrange("p (b j) -> p b j", b=8), G8), ALU.mult)
                    ins.then_inc(tb_d, 1)
            steps(e, step)
        tb_h = sem("inverse_parts_hi")

        h2h, h2l = f16c(64, 16), f16c(96, 16)
        rb = [f32(128 + 4 * s, TOK) for s in range(2)]
        f_r = sem("hidden_chunk")
        f_hi = sem("hidden_hi")
        od = [sem("output_stored_0"), sem("output_stored_1")]
        FB = {"f1": 0, "f2": 16, "f3": 32}

        def hidden_pe(e, name, sh, sl):
            pairs(e, H, lambda m, par, i, last: gemm_pe(e, name, m, par, sh, sl))

        def hidden_act(e, name, bias, dst):
            def chunk(m, par, i, last):
                split_next(e, "hi", name, m, par, i)
                e.wait_ge(w_used, used(name, m))
                e.wait_ge(acc_rd, m + (ACC0[name] + 1))
                e.activation(rb[par], bank(2 * par, 2), ACT.Relu, bias=bias[:, bass.ds(m, 1)],
                             scale=1.0 / W_SCALE).then_inc(f_r, 1)
                e.wait_ge(f_r, m + (FB[name] + 1))
                e.activation(chunk_of(dst, m), rb[par], ACT.Copy).then_inc(f_hi, 1)
            pairs(e, H, chunk)

        def hidden_dve(e, name, dsth, dstl):
            def chunk(m, par, i, last):
                split_next(e, "lo", name, m, par, i)
                e.wait_ge(f_hi, m + (FB[name] + 1))
                e.tensor_tensor(chunk_of(dstl, m), rb[par], chunk_of(dsth, m), ALU.subtract).then_inc(acc_rd, 1)
            pairs(e, H, chunk)

        def out_pe(e):
            pairs(e, KC, lambda m, par, i, last: gemm_pe(e, "f3", m, par, h2h, h2l))

        def out_act(e):
            def chunk(m, par, i, last):
                if not (last and par):
                    split_next(e, "hi", "f3", m, par, i)
                e.wait_ge(w_used, used("f3", m))
                e.wait_ge(acc_rd, m + (ACC0["f3"] + 1))
                if not (isinstance(m, int) and m < 2):
                    e.wait_ge(od[par], i * 16)
                e.activation(rb[par], bank(2 * par, 2), ACT.Identity, bias=b3c[:, bass.ds(m, 1)],
                             scale=1.0 / W_SCALE).then_inc(f_r, 1)
            pairs(e, KC, chunk, peel=1, peel_end=1)

        def out_dve(e):
            def chunk(m, par, i, last):
                if not (last and par):
                    split_next(e, "lo", "f3", m, par, i)
                e.wait_ge(f_r, m + (FB["f3"] + 1))
                e.tensor_tensor(rb[par], rb[par], x_chunk(m), ALU.add).then_inc(acc_rd, 1)
            pairs(e, KC, chunk, peel_end=1)

        def out_sp(e):
            u0 = UNIT0["f3"] + 2

            def chunk(m, par, i, last):
                if not (last and par):
                    for q in range(2):
                        e.wait_ge(w_rdy, m * 2 + (u0 + q - 1))
                        load_w(e, m * 2 + (u0 + q), q)
                e.wait_ge(acc_rd, acc_done("f3", m))
                e.dma_start(io["out"][:, bass.ds(m, 1), :].rearrange("p a n -> p (a n)"), rb[par]).then_inc(od[par], 16)
            pairs(e, KC, chunk, peel_end=1)
            for s in range(2):
                e.wait_ge(od[s], 64)

        block = ctx.enter_context(nc.Block())

        @block.sync
        def _(sp):
            start_sp(sp)
            xa_sp(sp)
            xb_sp(sp)
            xo_sp(sp)
            load_stream(sp, 18, UNIT0["dk"] + 2)
            dk_sp(sp)
            load_stream(sp, UNIT0["dk"] + 2, UNIT0["dv"] + 2)
            dv_sp(sp, UNIT0["dv"] + 2)
            load_stream(sp, UNIT0["dv"] + 16, UNIT0["f3"] + 2)
            out_sp(sp)

        @block.tensor
        def _(pe):
            start_pe(pe)
            xa_pe(pe)
            xb_pe(pe)
            pe.wait_ge(cl_lo, 32)
            residual_pe(pe, "xo", QR, QRL)
            ln_pe(pe, 1)
            dk_pe(pe)
            dq_pe(pe)
            dv_pe(pe)
            pe.wait_ge(ot_lo, 16)
            residual_pe(pe, "do", KH, KL)
            ln_pe(pe, 2)
            pe.wait_ge(ln_l, ln_done(2))
            hidden_pe(pe, "f1", xnh, xnl)
            pe.wait_ge(acc_rd, acc_done("f1", 15))
            hidden_pe(pe, "f2", r0h, r0l)
            pe.wait_ge(acc_rd, acc_done("f2", 15))
            out_pe(pe)

        @block.scalar
        def _(act):
            start_act(act)
            xa_act(act)
            xb_act(act)
            act.wait_ge(xr_ld, 16)
            residual_act(act, "xo", 1)
            dk_act(act)
            dq_act(act)
            dv_act(act)
            residual_act(act, "do", 2)
            act.wait_ge(ln_l, ln_done(2))
            hidden_act(act, "f1", b1c, r0h)
            hidden_act(act, "f2", b2c, h2h)
            out_act(act)

        @block.vector
        def _(dve):
            start_dve(dve)
            xa_dve(dve)
            xb_dve(dve)
            dve.wait_ge(xr_ld, 16)
            residual_dve(dve, "xo", 1)
            dk_dve(dve)
            dq_dve(dve)
            dv_dve(dve)
            residual_dve(dve, "do", 2)
            hidden_dve(dve, "f1", r0h, r0l)
            hidden_dve(dve, "f2", h2h, h2l)
            out_dve(dve)

        @block.gpsimd
        def _(pool):
            start_pool(pool)
            xa_pool(pool)
            xb_pool(pool)
            pool.wait_ge(xr_ld, 16)
            residual_pool(pool, "xo", 1)
            solve_pool(pool)
            dv_pool(pool)
            pool.wait_ge(ot_lo, 16)
            residual_pool(pool, "do", 2)


def _layouts(inputs):
    import numpy as np

    def a(name):
        return np.ascontiguousarray(inputs[name])

    def units(w):
        o, i = w.shape
        return w.reshape(o // P, P, i // 1024, 8, P).transpose(0, 2, 4, 3, 1).reshape(-1, P, 1024)

    t = np.float32
    out = {}
    out["xT"] = a("x").reshape(TOK, KC, P).transpose(2, 1, 0)
    out["wstream"] = np.concatenate([
        units(a("L0_xattn_Wq")), units(a("L0_xattn_Wo")), units(a("L0_attn_Wk").T), units(a("L0_attn_Wq").T),
        units(a("L0_attn_Wv").T), units(a("L0_attn_Wo").T), units(a("L0_ffn_W1")), units(a("L0_ffn_W2")),
        units(a("L0_ffn_W3"))])
    wqr = a("L0_xattn_W_qr").reshape(H, CJ, P, R).transpose(0, 2, 1, 3).reshape(H, P, CJ * R)
    out["abstream"] = np.concatenate([a("L0_xattn_w_kc_q"), wqr], axis=2)
    wkr = a("L0_xattn_W_kr").transpose(2, 0, 1)
    wkv = a("L0_xattn_w_kc_kv").reshape(H, P, 2, P).transpose(3, 0, 2, 1)
    out["wk"] = np.stack([np.concatenate([wkr, wkr]).reshape(P, H * DC), wkv.reshape(P, H * DC)])
    c = a("ctx_512")
    out["ctx"] = np.stack([c.reshape(NB, L, 2, P).transpose(0, 3, 2, 1).reshape(NB, P, TOK),
                           c.reshape(NB, 4, P, DC).transpose(0, 2, 1, 3).reshape(NB, P, TOK)])

    def rope(length, dim):
        inv = t(1.0) / t(10000.0) ** (np.arange(0, dim, 2, dtype=t) / t(dim))
        f = np.arange(length, dtype=t)[:, None] * inv[None, :]
        sin, cos = np.repeat(np.sin(f), 2, axis=-1), np.repeat(np.cos(f), 2, axis=-1)
        sign = np.where(np.arange(dim) < dim // 2, t(-1), t(1))
        return (sin * sign).astype(t), cos.astype(t)
    for name, tab in zip(("rsin", "rcos"), rope(S, CQ)):
        out[name] = (tab * t(1.0 / W_SCALE)).T.reshape(CJ, P, S).transpose(1, 0, 2)
    for name, tab in zip(("ksin", "kcos"), rope(L, DC)):
        out[name] = np.stack([tab.T.reshape(2, P, L).transpose(1, 0, 2).reshape(P, TOK),
                              tab.reshape(4, P, DC).transpose(1, 0, 2).reshape(P, TOK)])
    v = np.zeros((P, 256), t)
    v[:, 0:16] = a("L0_ffn_b1").reshape(16, P).T
    v[:, 16:32] = a("L0_ffn_b2").reshape(16, P).T
    v[:, 32:40] = a("L0_ffn_b3").reshape(8, P).T
    v[:, 40] = a("L0_attn_g_norm")
    for k, n in enumerate(("k", "q", "v")):
        v[:, 48 + 64 * k:112 + 64 * k] = a(f"L0_attn_conv_{n}").reshape(H, P, 4).transpose(1, 0, 2).reshape(P, 64)
    out["vecs"] = v
    out["wb"] = a("L0_attn_Wb").reshape(KC, P, H).transpose(1, 0, 2).reshape(P, P)
    seq, step = np.arange(P) // T, np.arange(P) % T
    out["ident"] = np.eye(P, dtype=t)
    out["ones"] = np.full((P, P), 1.0 / DM, t)
    out["same"] = (seq[:, None] == seq[None, :]).astype(t)
    out["upto"] = out["same"] * (step[:, None] <= step[None, :])
    out["lower"] = np.broadcast_to(np.tril(np.ones((T, T), t), -1)[None], (P, T, T))
    out["eye"] = np.broadcast_to(np.eye(T, dtype=t)[None], (P, T, T))
    return {k: np.ascontiguousarray(x.astype(t)) for k, x in out.items()}


def kernel(**inputs):
    import numpy as np
    import concourse.bacc as bacc
    from concourse.bass_utils import run_bass_kernel_spmd

    nc = bacc.Bacc("TRN2", target_bir_lowering=False, num_devices=1)
    arrays = _layouts(inputs)
    io = {n: nc.dram_tensor(n, x.shape, F32, kind="ExternalInput").ap() for n, x in arrays.items()}
    io["beta_s"] = nc.dram_tensor("beta_s", (H, TOK), F32, kind="Internal").ap()
    io["gram_s"] = nc.dram_tensor("gram_s", (H, G8, 8 * T * T), F32, kind="Internal").ap()
    io["inv_s"] = nc.dram_tensor("inv_s", (H, G8, 8 * T * T), F32, kind="Internal").ap()
    io["out"] = nc.dram_tensor("out", (P, KC, TOK), F32, kind="ExternalOutput").ap()
    build(nc, io)
    got = run_bass_kernel_spmd(nc, [arrays], core_ids=[0]).results[0]["out"]
    return np.ascontiguousarray(got.transpose(2, 1, 0)).reshape(16, 64, DM)
```

```python
from contextlib import ExitStack

import concourse.bass as bass
from concourse import mybir

F32 = mybir.dt.float32
F16 = mybir.dt.float16
ALU = mybir.AluOpType
ACT = mybir.ActivationFunctionType
AXX = mybir.AxisListType.X

P = 128
TOK = 1024
HALF = 512
DM = 1024
KC = DM // P
H = 16
NB = 16
S = 64
L = 512
DC = 256
CQ = 768
CJ = CQ // P
R = 64
T = 16
DB = 64
G8 = 8
W_SCALE = 256.0
QR_SCALE = 16.0
PR_SCALE = 4096.0
LN_EPS = 1e-5
KB = 1024

GEMMS = [("xq", 16, 1), ("xo", 8, 2), ("dk", 16, 1), ("dq", 16, 1), ("dv", 16, 1), ("do", 8, 2),
         ("f1", 16, 1), ("f2", 16, 2), ("f3", 8, 2)]
UNIT0, n = {}, 0
for name, chunks, per in GEMMS:
    UNIT0[name] = n
    n += chunks * per
UNITS = n


def one(ap):
    return ap.rearrange("p a n -> p (a n)")


def build(nc, io):
    ctx = ExitStack()
    with ctx:
        def sem(name):
            return ctx.enter_context(nc.semaphore(name))

        xid = ctx.enter_context(nc.sbuf_tensor("ident_sb", [P, P], F32))
        xones = ctx.enter_context(nc.sbuf_tensor("ones_sb", [P, P], F32))
        same = ctx.enter_context(nc.sbuf_tensor("same_sb", [P, P], F32))
        upto = ctx.enter_context(nc.sbuf_tensor("upto_sb", [P, P], F32))
        vecs = ctx.enter_context(nc.sbuf_tensor("vecs_sb", [P, 256], F32))
        onesm = ctx.enter_context(nc.sbuf_tensor("onesm", [P, 1], F32))
        small = ctx.enter_context(nc.sbuf_tensor("small", [P, 256], F32))
        wst = ctx.enter_context(nc.sbuf_tensor("wst", [P, 2, 1024], F32))
        whi = ctx.enter_context(nc.sbuf_tensor("whi", [P, 2, 1024], F16))
        wlo = ctx.enter_context(nc.sbuf_tensor("wlo", [P, 2, 1024], F16))
        arena = ctx.enter_context(nc.sbuf_tensor("arena", [P, 186 * 256], F32))

        def f32(kb, cols):
            a = int(kb * 256)
            return arena[:, a:a + cols]

        def f16(kb, cols):
            a = int(kb * 256)
            return arena[:, a:a + cols // 2].bitcast(F16)

        def f16c(kb, chunks):
            return f16(kb, chunks * TOK).rearrange("p (c n) -> p c n", n=TOK)

        ps = ctx.enter_context(nc.psum_tensor("ps", [P, 8, HALF], F32))

        def bank(b, k=1):
            return ps[:, b:b + k, :].rearrange("p a n -> p (a n)")

        r0h, r0l = f16c(0, 16), f16c(32, 16)
        xnh, xnl = f16c(64, 8), f16c(80, 8)
        b1c, b2c, b3c = vecs[:, 0:16], vecs[:, 16:32], vecs[:, 32:40]
        gno = vecs[:, 40:41]
        convw = {"dk": vecs[:, 48:112], "dq": vecs[:, 112:176], "dv": vecs[:, 176:240]}

        c_ld = sem("constants_loaded")
        ones_ld = sem("ones_loaded")
        w_ld = [sem("weights_loaded_0"), sem("weights_loaded_1")]
        w_hi = sem("weights_hi")
        w_rdy = sem("weights_split")
        w_used = sem("weights_used")
        acc_rd = sem("accumulator_read")

        def bc(ap, count, axis=1):
            shape = list(ap.shape)
            return ap.unsqueeze(axis).to_broadcast(shape[:axis] + [count] + shape[axis:])

        def load_w(e, u, s):
            e.dma_start(wst[:, s, :], one(io["wstream"][bass.ds(u, 1)].rearrange("a p n -> p a n"))).then_inc(w_ld[s], 16)

        def load_stream(e, u0, u1):
            with e.Fori(u0 // 2, u1 // 2) as i:
                for s in range(2):
                    e.wait_ge(w_rdy, i * 2 + (s - 1))
                    load_w(e, i * 2 + s, s)

        def split_hi(e, u, s, u2, first=False):
            e.wait_ge(w_ld[s], (u2 + 1) * 16)
            if not first:
                e.wait_ge(w_used, u - 1)
            e.activation(whi[:, s, :], wst[:, s, :], ACT.Copy, scale=W_SCALE).then_inc(w_hi, 1)

        def split_lo(e, u, s):
            e.wait_ge(w_hi, u + 1)
            e.scalar_tensor_tensor(out=wlo[:, s, :], in0=wst[:, s, :], scalar=W_SCALE, in1=whi[:, s, :],
                                   op0=ALU.mult, op1=ALU.subtract).then_inc(w_rdy, 1)

        def unit_mm(e, s, dst, sh, sl, k0, ks, first, last, inc):
            mm = None
            for k in ks:
                wh, wl = whi[:, s, k * P:k * P + P], wlo[:, s, k * P:k * P + P]
                for a, (w, x) in enumerate(((wh, sh), (wh, sl), (wl, sh))):
                    for c in range(2):
                        mm = e.matmul(dst[:, c * HALF:(c + 1) * HALF], w, x[:, k0 + k, c * HALF:(c + 1) * HALF],
                                      start=(first and k == ks[0] and a == 0),
                                      stop=(last and k == ks[-1] and a == 2))
            if inc:
                mm.then_inc(w_used, 1)

        PER = {name: per for name, _, per in GEMMS}
        ACC0 = {"xo": 0, "dk": 8, "dq": 24, "dv": 40, "do": 56, "f1": 64, "f2": 80, "f3": 96}

        def acc_done(name, m):
            return m + (ACC0[name] + 3)

        def used(name, m):
            return m * PER[name] + (UNIT0[name] + PER[name])

        def gemm_pe_first(e, name, before, sh, sl):
            e.wait_ge(acc_rd, acc_done(before, 14))
            for q in range(2):
                e.wait_ge(w_rdy, UNIT0[name] + q + 1)
                unit_mm(e, q, bank(0, 2), sh, sl, q * 8, range(8 - q), q == 0, False, q == 0)
            e.wait_ge(acc_rd, acc_done(before, 15))
            unit_mm(e, 1, bank(0, 2), sh, sl, 8, [7], False, True, True)

        def gemm_pe(e, name, m, par, sh, sl, parts=(0, 8), between=None):
            if parts[0] == 0:
                e.wait_ge(acc_rd, m + (ACC0[name] + 1))
            for q in range(PER[name]):
                s = (par * PER[name] + q) % 2
                if parts[0] == 0:
                    e.wait_ge(w_rdy, m * PER[name] + (UNIT0[name] + q + 1))
                unit_mm(e, s, bank(2 * par, 2), sh, sl, q * 8, list(range(*parts)), q == 0 and parts[0] == 0,
                        q == PER[name] - 1 and parts[1] == 8, parts[1] == 8)
                if q == 0 and between:
                    between()

        def split_next(e, what, name, m, par, i, which=(0, 1)):
            for q in which[:PER[name]]:
                s = (par * PER[name] + q) % 2
                u = m * PER[name] + (UNIT0[name] + q + 2)
                if what == "hi":
                    split_hi(e, u, s, (i if PER[name] == 1 else m) + (UNIT0[name] // 2 + 1))
                else:
                    split_lo(e, u, s)

        def pairs(e, n, body, peel=0, peel_end=0):
            def run(i, last):
                for par in range(2):
                    body(i * 2 + par, par, i, last)
            for i in range(peel):
                run(i, False)
            if n // 2 - peel - peel_end > 0:
                with e.Fori(peel, n // 2 - peel_end) as i:
                    run(i, False)
            for i in range(n // 2 - peel_end, n // 2):
                run(i, True)

        lnS, lnQ, lnX0, lnX1, lnM, lnV = (f32(96 + 4 * k, TOK) for k in range(6))
        lnX = [lnX0, lnX1]
        lnT = f32(120, 4 * TOK).rearrange("p (c n) -> p c n", n=TOK)
        lnE = f32(136, 2 * TOK).rearrange("p (c n) -> p c n", n=TOK)
        XT = f32(154, KC * TOK).rearrange("p (c n) -> p c n", n=TOK)
        sq_rdy = sem("squares")
        st_s = sem("sum_updated")
        st_q = sem("square_sum_updated")
        sq_used = sem("odd_squares_used")
        ln_mm = sem("ln_means")
        ln_a = sem("ln_scalar_steps")
        ln_v = sem("ln_vector_steps")
        ln_t = sem("ln_centred")
        ln_x = sem("ln_scaled")
        ln_h = sem("ln_hi")
        ln_l = sem("ln_lo")
        root = small[:, 48:49]
        LN_OF = {1: "xo", 2: "do"}

        def ln_done(z, c=KC - 1):
            return KC * z + (c + 3)

        def x_chunk(m):
            return one(XT[:, bass.ds(m, 1), :])

        def ln_wait_x(e, z, m):
            if z:
                e.wait_ge(acc_rd, acc_done(LN_OF[z], m))
            else:
                e.wait_ge(x_lds[m], 16)

        def ln_square(e, z, m, par):
            ln_wait_x(e, z, m)
            if z or (m and par == 0):
                e.wait_ge(st_q, m + 8 * z)
            elif m > 1:
                e.wait_ge(sq_used, m // 2)
            e.activation(lnX[par], x_chunk(m), ACT.Square).then_inc(sq_rdy, 1)

        def ln_sum(e, z, m):
            ln_wait_x(e, z, m)
            e.wait_ge(st_s, m + (8 * z + 1))
            e.tensor_tensor(lnS, lnS, x_chunk(m), ALU.add).then_inc(st_s, 1)

        def ln_square_sum(e, z, m, par):
            e.wait_ge(sq_rdy, m + (8 * z + 1))
            e.wait_ge(st_q, m + (8 * z + 1))
            e.tensor_tensor(lnQ, lnQ, lnX[par], ALU.add).then_inc(st_q, 1)

        def ln_mean(e, b, src, start=False, stop=False):
            for c in range(2):
                mm = e.matmul(bank(b + c), xones[:, :], src[:, c * HALF:(c + 1) * HALF], start=start, stop=stop)
            return mm

        def ln_pe_sums(e, z):
            e.wait_ge(st_s, 8 * z + 8)
            ln_mean(e, 4, lnS, start=True)
            e.wait_ge(st_q, 8 * z + 8)
            ln_mean(e, 6, lnQ, start=True)

        def ln_pe_last(e, z):
            ln_wait_x(e, z, KC - 1)
            ln_mean(e, 4, x_chunk(KC - 1), stop=True).then_inc(ln_mm, 1)
            e.wait_ge(sq_rdy, 8 * z + 8)
            ln_mean(e, 6, lnX[1], stop=True).then_inc(ln_mm, 1)

        def ln_act(e, z):
            e.activation(root, onesm[:, :], ACT.Sqrt)
            e.wait_ge(ln_mm, 2 * z + 1)
            e.activation(lnM, bank(4, 2), ACT.Copy).then_inc(ln_a, 1)
            e.activation(lnV, bank(4, 2), ACT.Square).then_inc(ln_a, 1)
            e.wait_ge(ln_v, 3 * z + 2)
            e.activation(lnX0, lnV, ACT.Sqrt).then_inc(ln_a, 1)
            for c in range(KC):
                e.wait_ge(ln_x, c + (8 * z + 1))
                e.activation(xnh[:, c, :], lnE[:, c % 2, :], ACT.Copy).then_inc(ln_h, 1)

        def ln_pool(e, z):
            e.wait_ge(ln_a, 3 * z + 1)
            for c in range(KC):
                if 8 * z + c - 3 > 0:
                    e.wait_ge(ln_x, 8 * z + c - 3)
                e.tensor_tensor(lnT[:, c % 4, :], XT[:, c, :], lnM, ALU.subtract).then_inc(ln_t, 1)

        def ln_dve(e, z):
            e.wait_ge(ln_mm, 2 * z + 2)
            e.wait_ge(ln_a, 3 * z + 2)
            e.tensor_tensor(lnV, bank(6, 2), lnV, ALU.subtract).then_inc(ln_v, 1)
            e.wait_ge(ln_v, 3 * z + 1)
            e.tensor_scalar(lnV, lnV, 0.0, LN_EPS, ALU.max, ALU.add).then_inc(ln_v, 1)
            e.wait_ge(ln_a, 3 * z + 3)
            e.reciprocal(lnV, lnX0).then_inc(ln_v, 1)
            e.wait_ge(ln_v, 3 * z + 3)

            def scale(c):
                e.wait_ge(ln_t, 8 * z + c + 1)
                e.wait_ge(ln_l, 8 * z + c + 1)
                e.tensor_tensor(lnE[:, c % 2, :], lnT[:, c % 4, :], lnV, ALU.mult).then_inc(ln_x, 1)

            def low(c):
                e.wait_ge(ln_h, 8 * z + c + 1)
                e.tensor_tensor(xnl[:, c, :], lnE[:, c % 2, :], xnh[:, c, :], ALU.subtract).then_inc(ln_l, 1)
            scale(0)
            for c in range(KC):
                if c < KC - 1:
                    scale(c + 1)
                low(c)

        def gemm_pe_ln(e, name, z):
            e.wait_ge(acc_rd, ACC0[name] + 2)
            e.wait_ge(w_rdy, UNIT0[name] + 2)
            for k in range(KC):
                e.wait_ge(ln_l, ln_done(z, k))
                for m in range(2):
                    unit_mm(e, m, bank(2 * m, 2), xnh, xnl, 0, [k], k == 0, k == KC - 1, k == KC - 1)

        x_lds = [sem(f"x_loaded_{c}") for c in range(KC)]
        cw = sem("conv_weights_scaled")

        def start_sp(e):
            e.dma_start(xones[:, :], io["ones"]).then_inc(ones_ld, 16)
            for c in range(KC):
                e.dma_start(XT[:, c, :], io["xT"][:, c, :]).then_inc(x_lds[c], 16)
                if c == 5:
                    for dst, src in ((xid, "ident"), (same, "same"), (upto, "upto"), (vecs, "vecs")):
                        e.dma_start(dst[:, :], io[src]).then_inc(c_ld, 16)
            load_w(e, 0, 0)
            load_w(e, 1, 1)

        def start_dve(e):
            for credit, n in ((acc_rd, 2), (ln_l, 2)):
                e.sem_inc(credit, n)
            e.memset(lnS, 0.0).then_inc(st_s, 1)
            e.memset(onesm[:, :], 1.0).then_inc(cw, 1)
            for c in range(KC - 1):
                ln_sum(e, 0, c)
            e.wait_ge(c_ld, 16 * 4)
            e.tensor_scalar(vecs[:, 48:240], vecs[:, 48:240], 1.0 / W_SCALE, None, ALU.mult).then_inc(cw, 1)

            split_lo(e, 0, 0)
            split_lo(e, 1, 1)
            ln_dve(e, 0)

        def start_act(e):
            for c in range(KC):
                ln_square(e, 0, c, c % 2)
            e.wait_ge(cw, 1)

            split_hi(e, 0, 0, 0, True)
            split_hi(e, 1, 1, 0, True)
            ln_act(e, 0)

        def start_pool(e):
            e.memset(lnQ, 0.0).then_inc(st_q, 1)
            for c in range(0, KC, 2):
                e.wait_ge(sq_rdy, c + 1)
                e.wait_ge(st_q, max(c, 1))
                e.tensor_tensor(lnQ, lnQ, lnX0, ALU.add).then_inc(st_q, 2 if c else 1)
            ln_pool(e, 0)

        def start_pe(e):
            e.wait_ge(ones_ld, 16)
            for c in (1, 3, 5):
                e.wait_ge(sq_rdy, c + 1)
                ln_mean(e, 6, lnX[1], start=(c == 1)).then_inc(sq_used, 1)
            e.wait_ge(st_s, 8)
            ln_mean(e, 4, lnS, start=True)
            e.wait_ge(x_lds[KC - 1], 16)
            ln_mean(e, 4, x_chunk(KC - 1), stop=True).then_inc(ln_mm, 1)
            e.wait_ge(st_q, 8)
            ln_mean(e, 6, lnQ)
            e.wait_ge(sq_rdy, 8)
            ln_mean(e, 6, lnX[1], stop=True).then_inc(ln_mm, 1)
            e.wait_ge(c_ld, 16 * 4)

        QR, QRL = r0h, r0l
        abst = f32(96, 1152)
        wcq = [[f16(101 + 4.5 * s + 1.5 * a, CQ) for a in range(2)] for s in range(2)]
        wqr = [f16(104 + 4.5 * s, CJ * P).rearrange("p (j a r) -> p j a r", j=CJ, a=2) for s in range(2)]
        rcos = f32(110, CJ * S).rearrange("p (j s) -> p j s", j=CJ)
        rsin = f32(112, CJ * S).rearrange("p (j s) -> p j s", j=CJ)
        qhl = [[f16((114, 182)[s] + 2 * k, TOK) for k in range(2)] for s in range(2)]
        rt = [[f32((118, 134, 166)[p] + 4 * k, TOK) for k in range(4)] for p in range(3)]
        ab_ld = sem("query_weights_loaded")
        rope_ld = sem("rotary_tables_loaded")
        wc_hi = sem("wide_query_weights_hi")
        wc_lo = sem("wide_query_weights_split")
        wr_hi = sem("q_r_weights_hi")
        wr_lo = sem("q_r_weights_split")
        q_hi = sem("query_hi")
        q_lo = sem("query_split")
        xc_mm = sem("wide_query_chunk")
        xc_rd = sem("wide_query_rotated")
        y_sum = sem("rotary_sum")
        y_hi = sem("rotary_hi")
        y_lo = [sem("rotary_split_0"), sem("rotary_split_1")]
        y_used = sem("rotary_used")
        qr_hi = sem("q_r_hi")
        qr_lo = sem("q_r_split")
        yh = [[f16(150 + 8 * s + 4 * k, TOK) for k in range(2)] for s in range(2)]
        yl = [[f16(152 + 8 * s + 4 * k, TOK) for k in range(2)] for s in range(2)]

        def load_ab(e, h):
            e.dma_start(abst, one(io["abstream"][bass.ds(h, 1)].rearrange("a p n -> p a n"))).then_inc(ab_ld, 16)

        def xa_sp(e):
            e.wait_ge(ln_mm, 2)
            load_ab(e, 0)
            e.wait_ge(ln_t, KC)
            e.dma_start(rcos, io["rcos"]).then_inc(rope_ld, 16)
            e.dma_start(rsin, io["rsin"]).then_inc(rope_ld, 16)

            def step(h, s):
                e.wait_ge(w_rdy, h)
                load_w(e, h + 1, s)
                e.wait_ge(wr_lo, h)
                load_ab(e, h)
            with e.Fori(0, 7) as i:
                step(i * 2 + 1, 0)
                step(i * 2 + 2, 1)
            step(15, 0)
            e.wait_ge(w_rdy, 16)
            load_w(e, 17, 1)

        def qr_pe(e, h, hs, p):
            P3, s = h * 3 + p, (hs + p) % 2
            if p == 0:
                if not (isinstance(h, int) and h == 0):
                    e.wait_ge(qr_lo, h)
                e.wait_ge(wr_lo, h + 1)
            for part in range(2):
                e.wait_ge(y_lo[part], P3 + 1)
            for k in range(2):
                w = wqr[hs][:, p + 3 * k, :, :].rearrange("p a r -> p (a r)")
                for a, y in enumerate((yh[s][k], yl[s][k])):
                    for c in range(2):
                        mm = e.matmul(bank(6 + c), w, y[:, c * HALF:(c + 1) * HALF], start=(p == 0 and k == 0 and a == 0),
                                      stop=(p == 2 and k == 1 and a == 1))
            mm.then_inc(y_used, 1)

        KSL = [(0, 4), (4, 6), (6, 8)]

        def heads(e, head):
            for h in (0, 1):
                head(h, h, 0)
            with e.Fori(1, 7) as i:
                for hs in range(2):
                    head(i * 2 + hs, hs, i)
            for h in (14, 15):
                head(h, h - 14, 7)

        def xa_pe(e):
            def gemm(h, s, k0, k1):
                if k0 == 0:
                    e.wait_ge(w_rdy, h + 1)
                unit_mm(e, s, bank(0, 2), xnh, xnl, 0, list(range(k0, k1)), k0 == 0, k1 == 8, k1 == 8)

            def head(h, hs, i):
                first, last = isinstance(h, int) and h == 0, isinstance(h, int) and h == 15
                for p in range(3):
                    P3 = h * 3 + p
                    if p == 0:
                        e.wait_ge(q_lo, h + 1)
                        e.wait_ge(wc_lo, h + 1)
                    if not last:
                        gemm(h + 1, 1 - hs, *KSL[p])
                    for k in range(2):
                        if not (first and p == 0):
                            e.wait_ge(xc_rd, P3 * 2 + (k - 1))
                        j = p + 3 * k
                        wh, wl = (wcq[hs][a][:, j * P:(j + 1) * P] for a in range(2))
                        for a, (w, x) in enumerate(((wh, qhl[hs][0]), (wh, qhl[hs][1]), (wl, qhl[hs][0]))):
                            for c in range(2):
                                mm = e.matmul(bank(2 + 2 * k + c), w, x[:, c * HALF:(c + 1) * HALF],
                                              start=(a == 0), stop=(a == 2))
                        mm.then_inc(xc_mm, 1)
                    if not first:
                        qr_pe(e, h - 1, 1 - hs, p)
            e.wait_ge(w_rdy, 1)
            for k in range(KC):
                e.wait_ge(ln_l, ln_done(0, k))
                unit_mm(e, 0, bank(0, 2), xnh, xnl, 0, [k], k == 0, k == KC - 1, k == KC - 1)
            heads(e, head)
            for p in range(3):
                qr_pe(e, 15, 1, p)

        def xa_order(e, wide, narrow, q, weights, rotate, y, qr, wk0, tail):
            def head(h, hs, i):
                early = isinstance(h, int) and h < 2
                first, last = isinstance(h, int) and h == 0, isinstance(h, int) and h == 15
                for p in range(3):
                    P3, s = h * 3 + p, (hs + p) % 2
                    if p == 0 and not early:
                        qr(h - 2)
                    if p < 2:
                        rotate(p, P3, first)
                    if not (first and p < 2):
                        y(P3 - 2, s, (p + 1) % 3, early and P3 < 4)
                    if p == 0:
                        narrow(h, hs)
                    if last and p:
                        for piece in (p * 2 - 2, p * 2 - 1):
                            wk0(piece)
                    if p == 1:
                        weights(h, hs, i)
                        if not last:
                            wide(h + 1, 1 - hs)
                    if p == 2:
                        if not last:
                            q(h + 1, 1 - hs)
                        rotate(p, P3, first)
            wide(0, 0)
            q(0, 0)
            heads(e, head)
            y(46, 0, 1, False)
            qr(14)
            y(47, 1, 2, False)
            tail()
            qr(15)

        def xa_act(e):
            def wide(h, hs):
                e.wait_ge(ab_ld, h * 16 + 16)
                e.activation(wcq[hs][0], abst[:, 0:CQ], ACT.Copy, scale=W_SCALE).then_inc(wc_hi, 1)

            def narrow(h, hs):
                e.activation(wqr[hs][:, :, 0, :], abst[:, CQ:].rearrange("p (j r) -> p j r", j=CJ), ACT.Copy,
                             scale=W_SCALE).then_inc(wr_hi, 1)

            def q(h, hs):
                e.wait_ge(w_used, h + 1)
                e.activation(qhl[hs][0], bank(0, 2), ACT.Copy, scale=1.0 / W_SCALE).then_inc(q_hi, 1)

            def weights(h, s, i):
                split_hi(e, h + 2, s, i + 1)

            def y(P3, s, p, first):
                e.wait_ge(y_sum, P3 * 2 + 2)
                if not first:
                    e.wait_ge(y_used, P3 - 1)
                for k in range(2):
                    e.activation(yh[s][k], rt[p][2 * k], ACT.Copy).then_inc(y_hi, 1)

            def qr(h):
                e.wait_ge(y_used, h * 3 + 3)
                e.activation(one(QR[:, bass.ds(h, 1), :]), bank(6, 2), ACT.Copy,
                             scale=QR_SCALE / W_SCALE).then_inc(qr_hi, 1)
            xa_order(e, wide, narrow, q, weights, lambda *a: None, y, qr, lambda n: wk_hi_part(e, 0, n), lambda: None)

        def xa_dve(e):
            def wide(h, hs):
                e.wait_ge(wc_hi, h + 1)
                e.scalar_tensor_tensor(out=wcq[hs][1], in0=abst[:, 0:CQ], scalar=W_SCALE, in1=wcq[hs][0],
                                       op0=ALU.mult, op1=ALU.subtract).then_inc(wc_lo, 1)

            def narrow(h, hs):
                e.wait_ge(wr_hi, h + 1)
                e.scalar_tensor_tensor(out=wqr[hs][:, :, 1, :], in0=abst[:, CQ:].rearrange("p (j r) -> p j r", j=CJ),
                                       scalar=W_SCALE, in1=wqr[hs][:, :, 0, :],
                                       op0=ALU.mult, op1=ALU.subtract).then_inc(wr_lo, 1)

            def q(h, hs):
                e.wait_ge(q_hi, h + 1)
                e.scalar_tensor_tensor(out=qhl[hs][1], in0=bank(0, 2), scalar=1.0 / W_SCALE, in1=qhl[hs][0],
                                       op0=ALU.mult, op1=ALU.subtract).then_inc(q_lo, 1)

            def weights(h, s, i):
                split_lo(e, h + 2, s)

            def rotate(p, P3, first):
                if not first:
                    for part in range(2):
                        e.wait_ge(y_lo[part], P3 - 2)
                for k in range(2):
                    j, other = p + 3 * k, p + 3 * (1 - k)
                    e.wait_ge(xc_mm, P3 * 2 + (k + 1))
                    x = bank(2 + 2 * k, 2).rearrange("p (b s) -> p b s", s=S)
                    for dst, table in ((rt[p][2 * k], rcos[:, j, :]), (rt[p][2 * k + 1], rsin[:, other, :])):
                        ins = e.tensor_tensor(dst.rearrange("p (b s) -> p b s", s=S), x, bc(table, NB), ALU.mult)
                    ins.then_inc(xc_rd, 1)

            def y(P3, s, p, first):
                e.wait_ge(y_hi, P3 * 2 + 1)
                e.tensor_tensor(yl[s][0], rt[p][0], yh[s][0], ALU.subtract).then_inc(y_lo[0], 1)

            def qr(h):
                e.wait_ge(qr_hi, h + 1)
                e.scalar_tensor_tensor(out=one(QRL[:, bass.ds(h, 1), :]), in0=bank(6, 2), scalar=QR_SCALE / W_SCALE,
                                       in1=one(QR[:, bass.ds(h, 1), :]), op0=ALU.mult, op1=ALU.subtract).then_inc(qr_lo, 1)
            e.wait_ge(rope_ld, 32)

            xa_order(e, wide, narrow, q, weights, rotate, y, qr, lambda n: wk_lo_part(e, 0, n), lambda: kmul(e, 0, 0))

        def xa_pool(e):
            def low(P3, s, p):
                e.wait_ge(y_hi, P3 * 2 + 2)
                e.tensor_tensor(yl[s][1], rt[p][2], yh[s][1], ALU.subtract).then_inc(y_lo[1], 1)

            def head(h, hs, i):
                for p in range(3):
                    P3, s = h * 3 + p, (hs + p) % 2
                    if not (isinstance(h, int) and P3 < 2):
                        low(P3 - 2, s, (p + 1) % 3)
                    e.wait_ge(xc_rd, P3 * 2 + 2)
                    for k in range(2):
                        e.tensor_tensor(rt[p][2 * k], rt[p][2 * k], rt[p][3 - 2 * k], ALU.add).then_inc(y_sum, 1)
            heads(e, head)
            low(46, 0, 1)
            low(47, 1, 2)

        wk = [[f16((64, 96)[a] + 8 * k, H * DC).rearrange("p (h d) -> p h d", d=DC) for k in range(2)] for a in range(2)]
        wkst = [[f32(80 + 4 * n, TOK) for n in range(4)], [f32(k, TOK) for k in (152, 156, 176, 180)]]
        QA_PARTS = [(0, 0), (0, 1), (1, 1), (1, 0)]
        QA = [[[f16(112 + 8 * s + 4 * d + 2 * k, TOK) for k in range(2)] for d in range(2)] for s in range(2)]
        kcos, ksin = [f32(80, TOK), f32(88, TOK)], [f32(84, TOK), f32(92, TOK)]
        kvst = [f32(128, TOK), f32(132, TOK)]
        km1, km2 = f32(136, TOK), f32(140, TOK)
        KV = [[[f16(144 + 8 * s + 4 * l + 2 * k, TOK) for k in range(2)] for l in range(2)] for s in range(2)]
        CC = [[f16(160 + 2 * d + k, HALF) for k in range(2)] for d in range(2)]
        ex_t = [f32(164 + 2 * s, L) for s in range(2)]
        AT = [[f16(168 + 8 * s + 4 * k, 4 * L).rearrange("p (c n) -> p c n", c=4) for k in range(2)] for s in range(2)]
        nmax, rsum, rinv = small[:, 0:2], small[:, 2:4], small[:, 4:6]
        wk_ld = [sem("score_weights_loaded"), sem("value_weights_loaded")]
        wk_hi = sem("key_value_weights_hi")
        wk_lo = sem("key_value_weights_split")
        kt_ld = sem("key_tables_loaded")
        kv_ld = [sem("context_loaded"), sem("context_rows_loaded")]
        kv_mul = sem("context_rotated")
        kv_sum = sem("context_rotary_sum")
        kv_hi = sem("context_hi")
        kv_lo = sem("context_split")
        qa_mm = sem("q_a_ready")
        qa_hi = sem("q_a_hi")
        qa_lo = sem("q_a_split")
        sc_mm = sem("scores_ready")
        mx = sem("scores_maximum")
        exd = sem("scores_exp")
        rcp = sem("weights_sum_inverse")
        nrm = sem("attention_normalised")
        tr_mm = sem("attention_transposed")
        at_hi = sem("attention_hi")
        at_lo = sem("attention_split")
        cc_mm = sem("mean_context_ready")
        cc_hi = sem("mean_context_hi")
        cc_lo = sem("mean_context_split")
        cl_mm = sem("values_ready")
        cl_hi = sem("values_hi")
        cl_lo = sem("values_split")

        def wk_part(t, n):
            return t[:, 4 * n:4 * n + 4, :].rearrange("p h d -> p (h d)")

        def wk_hi_part(e, a, n):
            if n == 0:
                e.wait_ge(wk_ld[a], 64)
            e.activation(wk_part(wk[a][0], n), wkst[a][n], ACT.Copy, scale=W_SCALE).then_inc(wk_hi, 1)

        def wk_lo_part(e, a, n):
            e.wait_ge(wk_hi, 4 * a + n + 1)
            e.scalar_tensor_tensor(out=wk_part(wk[a][1], n), in0=wkst[a][n], scalar=W_SCALE, in1=wk_part(wk[a][0], n),
                                   op0=ALU.mult, op1=ALU.subtract).then_inc(wk_lo, 1)

        def kmul(e, b, l):
            if isinstance(b, int) and b == 0:
                e.wait_ge(kt_ld, 64)
            e.wait_ge(kv_ld[l], b * 16 + 16)
            if not (isinstance(b, int) and b == 0 and l == 0):
                e.wait_ge(kv_lo, b * 2 + l)
            e.tensor_tensor(km1, kvst[l], kcos[l], ALU.mult)
            sh = (lambda t: t.rearrange("p (c a n) -> p c a n", a=2, n=(L, P)[l]))
            for a in range(2):
                ins = e.tensor_tensor(sh(km2)[:, :, a, :], sh(kvst[l])[:, :, 1 - a, :], sh(ksin[l])[:, :, a, :], ALU.mult)
            ins.then_inc(kv_mul, 1)

        def klow(e, b, s, l):
            e.wait_ge(kv_hi, b * 2 + (l + 1))
            e.tensor_tensor(KV[s][l][1], km1, KV[s][l][0], ALU.subtract).then_inc(kv_lo, 1)

        def xb_sp(e):
            e.wait_ge(w_used, 16)
            for n in range(4):
                e.dma_start(wkst[0][n], io["wk"][0, :, n * TOK:(n + 1) * TOK]).then_inc(wk_ld[0], 16)
            e.wait_ge(wk_lo, 4)
            for l in range(2):
                e.dma_start(kcos[l], io["kcos"][l]).then_inc(kt_ld, 16)
                e.dma_start(ksin[l], io["ksin"][l]).then_inc(kt_ld, 16)
            for part in range(2):
                e.wait_ge(y_lo[part], 47)
            for l in range(2):
                e.dma_start(kvst[l], io["ctx"][l, 0]).then_inc(kv_ld[l], 16)
            for part in range(2):
                e.wait_ge(y_lo[part], 48)
            e.wait_ge(y_used, 48)
            for n in range(4):
                e.dma_start(wkst[1][n], io["wk"][1, :, n * TOK:(n + 1) * TOK]).then_inc(wk_ld[1], 16)
            with e.Fori(1, NB) as b:
                for l in range(2):
                    e.wait_ge(kv_mul, b * 2 + (l - 1))
                    e.dma_start(kvst[l], one(io["ctx"][l, bass.ds(b, 1)].rearrange("a p n -> p a n"))).then_inc(kv_ld[l], 16)

        def xb_pe(e):
            def qa(b, s, n, early=False):
                d, half = QA_PARTS[n]
                if early == "start":
                    if d:
                        e.wait_ge(qa_lo, half + 1)
                elif n == 3 and not early:
                    e.wait_ge(cl_lo, b * 2 - 3)
                elif n == 3:
                    e.wait_ge(qa_lo, b * 4 + 1)
                elif n != 1:
                    e.wait_ge(qa_lo, b * 4 + n)
                for h in range(8):
                    for a, (w, x) in enumerate(((0, QR), (0, QRL), (1, QR))):
                        mm = e.matmul(bank(6 + half)[:, h * S:(h + 1) * S],
                                      wk[0][w][:, half * 8 + h, d * P:(d + 1) * P],
                                      x[:, half * 8 + h, bass.ds(b * S, S)], start=(a == 0), stop=(a == 2))
                mm.then_inc(qa_mm, 1)

            def scores(b, s, r, start):
                if r == 0:
                    e.wait_ge(kv_lo, b * 2 + 1)
                    e.wait_ge(qa_lo, b * 4 + 4)
                if not (start and r < 2):
                    e.wait_ge(exd, b * 8 + (r - 1))
                n = 0
                for d in range(2):
                    for w, x in ((0, 0), (0, 1), (1, 0)):
                        mm = e.matmul(bank(2 + r % 2), QA[s][d][w][:, r * P:(r + 1) * P],
                                      KV[s][0][x][:, d * L:(d + 1) * L], start=(n == 0), stop=(n == 5))
                        n += 1
                mm.then_inc(sc_mm, 1)

            def trans(tile, par, early):
                e.wait_ge(nrm, tile + 1)
                if not early:
                    e.wait_ge(at_lo, tile - 1)
                for c in range(4):
                    mm = e.transpose(bank(4 + par)[:, c * P:(c + 1) * P], ex_t[par][:, c * P:(c + 1) * P], xid[:, :])
                mm.then_inc(tr_mm, 1)

            def cc(G, g, s, d, early):
                if not early:
                    e.wait_ge(cc_lo, G * 2 + (d - 1))
                e.wait_ge(at_lo, G * 4 + 4)
                e.wait_ge(kv_lo, (G - g) + 2)
                n = 0
                for c in range(4):
                    for w, x in ((0, 0), (0, 1), (1, 0)):
                        mm = e.matmul(bank(d), KV[s][1][w][:, c * DC + d * P:c * DC + (d + 1) * P], AT[g][x][:, c, :],
                                      start=(n == 0), stop=(n == 11))
                        n += 1
                mm.then_inc(cc_mm, 1)

            def cl(G, g, last):
                e.wait_ge(cc_lo, G * 2 + 2)
                if last == "end":
                    e.wait_ge(cl_lo, G - 1)
                else:
                    e.wait_ge(qa_lo, 64 if last else G * 2 + 9)
                for h in range(8):
                    n = 0
                    for d in range(2):
                        for w, x in ((0, 0), (0, 1), (1, 0)):
                            mm = e.matmul(bank(6 + g)[:, h * S:(h + 1) * S], wk[1][w][:, 8 * g + h, d * P:(d + 1) * P],
                                          CC[d][x][:, h * S:(h + 1) * S], start=(n == 0), stop=(n == 5))
                            n += 1
                mm.then_inc(cl_mm, 1)

            def batch(b, s, first=False, last=False):
                for r in range(8):
                    if r in (0, 4) and not last:
                        qa(b + 1, 1 - s, r // 2, first)
                    scores(b, s, r, first)
                    if r in (0, 4) and not last:
                        qa(b + 1, 1 - s, r // 2 + 1, first)
                    if r in (1, 5) and not first:
                        cl(b * 2 - 2 + r // 4, r // 4, last)
                    if r in (2, 3) and not first:
                        cc(b * 2 - 1, 1, 1 - s, r - 2, False)
                    if r in (6, 7):
                        cc(b * 2, 0, s, r - 6, first)
                    if not (first and r == 0):
                        trans(b * 8 + (r - 1), (r - 1) % 2, first and r < 3)
            e.wait_ge(wk_lo, 4)
            e.wait_ge(qr_lo, 16)
            for q in range(4):
                qa(0, 0, q, "start")
            batch(0, 0, first=True)
            e.wait_ge(wk_lo, 8)
            with e.Fori(0, 7) as i:
                batch(i * 2 + 1, 1)
                batch(i * 2 + 2, 0)
            batch(15, 1, last=True)
            trans(127, 1, False)
            cl(30, 0, "end")
            cc(31, 1, 1, 0, False)
            cc(31, 1, 1, 1, False)
            cl(31, 1, "end")

        def xb_order(e, exp_, norm, attn, mean, vals, qa, kmul, khi, klo, wk1):
            def batch(b, s, first=False, last=False):
                for r in range(8):
                    if not (first and r < 2):
                        q = (r - 2) % 8
                        attn(b * 8 + (r - 2), q % 2, q // 4, q % 4)
                    if r in (0, 4) and not first:
                        mean(b * 2 - 2 + r // 4, 1)
                    if r in (2, 6) and not first:
                        vals(b * 2 - 2 + r // 4, r // 4, b - 1)
                    if r == 3 and not first:
                        mean(b * 2 - 1, 0)
                    if r == 7:
                        mean(b * 2, 0)
                    if r in (0, 4) and not last:
                        qa(b + 1, 1 - s, r // 2)
                    if r in (1, 5) and not last:
                        qa(b + 1, 1 - s, r // 2 + 1)
                    exp_(b * 8 + r, r % 2, first and r < 2)
                    if first and r == 0:
                        klo(0, 0, 1)
                    norm(b * 8 + r, r % 2)
                    if r in (3, 7) and not last:
                        khi(b + 1, 1 - s, r // 7)
                    if first and r < 4:
                        wk1(r)
            khi(0, 0, 0)
            for q in range(2):
                qa(0, 0, q)
            klo(0, 0, 0)
            for q in range(2, 4):
                qa(0, 0, q)
            kmul(0, 1)
            khi(0, 0, 1)
            batch(0, 0, first=True)
            with e.Fori(0, 7) as i:
                batch(i * 2 + 1, 1)
                batch(i * 2 + 2, 0)
            batch(15, 1, last=True)
            attn(126, 0, 1, 2)
            mean(30, 1)
            attn(127, 1, 1, 3)
            vals(30, 0, 15)
            mean(31, 0)
            mean(31, 1)
            vals(31, 1, 15)

        def batch_cols(t, g, b):
            return t[:, 8 * g:8 * g + 8, bass.ds(b * S, S)]

        def xb_act(e):
            def exp_(tile, par, early):
                e.wait_ge(mx, tile + 1)
                if not early:
                    e.wait_ge(tr_mm, tile - 1)
                e.activation(ex_t[par], bank(2 + par), ACT.Exp, bias=nmax[:, par:par + 1],
                             accum_out=rsum[:, par:par + 1]).then_inc(exd, 1)

            def attn(tile, par, g, q):
                e.wait_ge(tr_mm, tile + 1)
                e.activation(AT[g][0][:, :, q * P:(q + 1) * P], bank(4 + par).rearrange("p (c n) -> p c n", c=4),
                             ACT.Copy).then_inc(at_hi, 1)

            def mean(G, d):
                e.wait_ge(cc_mm, G * 2 + (d + 1))
                e.activation(CC[d][0], bank(d), ACT.Copy, scale=1.0 / PR_SCALE).then_inc(cc_hi, 1)

            def vals(G, g, b):
                e.wait_ge(cl_mm, G + 1)
                e.activation(batch_cols(QR, g, b), bank(6 + g).rearrange("p (h s) -> p h s", s=S), ACT.Copy,
                             scale=1.0 / W_SCALE).then_inc(cl_hi, 1)

            def qa(b, s, n):
                d, half = QA_PARTS[n]
                e.wait_ge(qa_mm, b * 4 + (n + 1))
                e.activation(QA[s][d][0][:, half * HALF:(half + 1) * HALF], bank(6 + half), ACT.Copy,
                             scale=1.0 / (W_SCALE * QR_SCALE)).then_inc(qa_hi, 1)

            def khi(b, s, l):
                e.wait_ge(kv_sum, b * 2 + (l + 1))
                e.activation(KV[s][l][0], km1, ACT.Copy).then_inc(kv_hi, 1)
            none = lambda *a: None
            e.wait_ge(qr_lo, 16)
            xb_order(e, exp_, none, attn, mean, vals, qa, none, khi, none, lambda n: wk_hi_part(e, 1, n))

        def xb_dve(e):
            def exp_(tile, par, early):
                e.wait_ge(sc_mm, tile + 1)
                e.tensor_reduce(nmax[:, par:par + 1], bank(2 + par), AXX, ALU.max, negate=True).then_inc(mx, 1)

            def norm(tile, par):
                e.wait_ge(exd, tile + 1)
                e.reciprocal(rinv[:, par:par + 1], rsum[:, par:par + 1]).then_inc(rcp, 1)
                e.wait_ge(rcp, tile + 1)
                e.tensor_scalar(ex_t[par], ex_t[par], rinv[:, par:par + 1], PR_SCALE, ALU.mult, ALU.mult).then_inc(nrm, 1)

            def attn(tile, par, g, q):
                e.wait_ge(at_hi, tile + 1)
                a, src = AT[g], bank(4 + par).rearrange("p (c n) -> p c n", c=4)
                e.tensor_tensor(a[1][:, :, q * P:(q + 1) * P], src, a[0][:, :, q * P:(q + 1) * P],
                                ALU.subtract).then_inc(at_lo, 1)

            def mean(G, d):
                e.wait_ge(cc_hi, G * 2 + (d + 1))
                e.scalar_tensor_tensor(out=CC[d][1], in0=bank(d), scalar=1.0 / PR_SCALE, in1=CC[d][0],
                                       op0=ALU.mult, op1=ALU.subtract).then_inc(cc_lo, 1)

            def vals(G, g, b):
                e.wait_ge(cl_hi, G + 1)
                e.scalar_tensor_tensor(out=batch_cols(QRL, g, b), in0=bank(6 + g).rearrange("p (h s) -> p h s", s=S),
                                       scalar=1.0 / W_SCALE, in1=batch_cols(QR, g, b),
                                       op0=ALU.mult, op1=ALU.subtract).then_inc(cl_lo, 1)

            def qa(b, s, n):
                d, half = QA_PARTS[n]
                e.wait_ge(qa_hi, b * 4 + (n + 1))
                c = slice(half * HALF, (half + 1) * HALF)
                e.scalar_tensor_tensor(out=QA[s][d][1][:, c], in0=bank(6 + half), scalar=1.0 / (W_SCALE * QR_SCALE),
                                       in1=QA[s][d][0][:, c], op0=ALU.mult, op1=ALU.subtract).then_inc(qa_lo, 1)

            xb_order(e, exp_, norm, attn, mean, vals, qa, lambda *a: kmul(e, *a), lambda *a: None,
                     lambda *a: klow(e, *a),
                     lambda n: wk_lo_part(e, 1, n))

        def xb_pool(e):
            def total(b, l):
                e.wait_ge(kv_mul, b * 2 + (l + 1))
                e.tensor_tensor(km1, km1, km2, ALU.add).then_inc(kv_sum, 1)

            def context(b, s):
                for l in range(2):
                    kmul(e, b, l)
                    total(b, l)
                    klow(e, b, s, l)
            total(0, 0)
            total(0, 1)
            with e.Fori(0, 7) as i:
                context(i * 2 + 1, 1)
                context(i * 2 + 2, 0)
            context(15, 1)

        def residual_pe(e, name, z, sh, sl):
            def chunk(m, par, i, last):
                if name == "do" and isinstance(m, int) and m == 0:
                    return
                gemm_pe(e, name, m, par, sh, sl, between=(lambda: ln_pe_sums(e, z)) if last and par else None)
            pairs(e, KC, chunk, peel=1, peel_end=1)
            ln_pe_last(e, z)

        def residual_act(e, name, z):
            def chunk(m, par, i, last):
                split_next(e, "hi", name, m, par, i)
                ln_square(e, z, m, par)
            pairs(e, KC, chunk)
            ln_act(e, z)

        def residual_dve(e, name, z):
            def chunk(m, par, i, last):
                split_next(e, "lo", name, m, par, i, (0,))
                e.wait_ge(w_used, used(name, m))
                e.scalar_tensor_tensor(out=x_chunk(m), in0=bank(2 * par, 2), scalar=1.0 / W_SCALE, in1=x_chunk(m),
                                       op0=ALU.mult, op1=ALU.add).then_inc(acc_rd, 1)
                split_next(e, "lo", name, m, par, i, (1,))
            pairs(e, KC, chunk)
            ln_dve(e, z)

        def residual_pool(e, name, z):
            e.memset(lnS, 0.0).then_inc(st_s, 1)
            e.memset(lnQ, 0.0).then_inc(st_q, 1)

            def chunk(m, par, i, last):
                if not (last and par):
                    ln_sum(e, z, m)
                    ln_square_sum(e, z, m, par)
            pairs(e, KC, chunk, peel_end=1)
            ln_pool(e, z)

        def xo_sp(e):
            e.wait_ge(cl_lo, 32)
            e.dma_start(XT, io["xT"]).then_inc(xr_ld, 16)
            for dst, src in ((lower, "lower"), (eye, "eye"), (wbst, "wb")):
                e.dma_start(dst, io[src]).then_inc(d_ld, 16)
        xr_ld = sem("x_reloaded")

        KH, KL = r0h, r0l
        yc = f32(96, TOK)
        sv = [f32(100 + 4 * s, TOK) for s in range(2)]
        gm = f32(108, TOK)
        qdh, qdl = f16(112, TOK), f16(114, TOK)
        qsq = f32(116, TOK)
        sA = f32(120, 2048).rearrange("p (h i j) -> p h i j", h=8, i=T)
        sT = f32(128, 2048).rearrange("p (h i j) -> p h i j", h=8, i=T)
        sU = f32(136, 2048).rearrange("p (h i j) -> p h i j", h=8, i=T)
        lower = f32(144, 256).rearrange("p (i j) -> p i j", i=T)
        eye = f32(145, 256).rearrange("p (i j) -> p i j", i=T)
        gc = [f32(146 + s / 2, P).rearrange("p (g j) -> p g j", g=G8) for s in range(2)]
        betaq = f32(147, P).rearrange("p (h t) -> p h t", h=8)
        rk = f32(147.5, P).rearrange("p (h t) -> p h t", h=8)
        rkb = f32(148, P).rearrange("p (h t) -> p h t", h=8)
        nhalf = f32(148.5, P).rearrange("p (h t) -> p h t", h=8)
        q2e = f32(149, P)
        beta = f32(149.5, TOK)[0:H, :]
        wbh, wbl = f16(147, P), f16(147.25, P)
        wbst = f32(153.5, P)
        d_ld = sem("delta_constants_loaded")
        wb_hi = sem("beta_weights_hi")
        wb_lo = sem("beta_weights_split")
        b_mm = sem("beta_ready")
        b_sg = sem("beta_sigmoid")
        b_st = sem("beta_stored")
        seq_ld = sem("sequences_loaded")
        cv = sem("conv_first_taps")
        cy = sem("conv_last_tap_input")
        si = sem("silu")
        k_hi = sem("key_hi")
        k_lo = sem("key_split")
        g_mm = sem("gram_ready")
        g_ms = sem("gram_masked")
        g_c = sem("gram_compact")
        g_st = [sem("gram_stored_0"), sem("gram_stored_1")]
        pr = sem("solve_prepared")
        sl_u = sem("solve_product")
        sl_t = sem("solve_row")
        tc_st = sem("inverse_stored")
        q_h2 = sem("delta_query_hi")
        q_sq = sem("delta_query_square")
        q_l2 = sem("delta_query_split")
        p_mm = sem("products_ready")
        p_ms = sem("products_masked")
        p_hi = sem("products_hi")
        p_lo = sem("products_split")
        q2_rd = sem("query_norms")
        BASE = {"dk": 0, "dq": 16, "dv": 32}

        def conv_act(e, name, m, par, between=None):
            e.wait_ge(w_used, used(name, m))
            if not (isinstance(m, int) and m == 0 and name == "dk"):
                e.wait_ge(si, m + BASE[name])
            e.activation(yc, bank(2 * par, 2), ACT.Copy, scale=convw[name][:, bass.ds(m * 4 + 3, 1)]).then_inc(cy, 1)
            if between:
                between()
            e.wait_ge(acc_rd, acc_done(name, m))
            e.activation(sv[par].rearrange("p (b t) -> p t b", t=T), yc.rearrange("p (t b) -> p t b", t=T),
                         ACT.Silu).then_inc(si, 1)

        def conv_dve(e, name, m, par):
            e.wait_ge(cy, m + (BASE[name] + 1))
            for back in (1, 2, 3):
                n = TOK - DB * back
                if back > 1:
                    e.wait_ge(cv, m * 2 + (BASE[name] * 2 + back - 1))
                e.scalar_tensor_tensor(out=yc[:, DB * back:], in0=bank(2 * par, 2)[:, 0:n],
                                       scalar=convw[name][:, bass.ds(m * 4 + (3 - back), 1)], in1=yc[:, DB * back:],
                                       op0=ALU.mult, op1=ALU.add).then_inc(acc_rd if back == 3 else cv, 1)

        def blocks(e, dst, w, x, inc):
            for g in range(G8):
                cols = slice(g * P, (g + 1) * P)
                for a, (i, j) in enumerate(((0, 0), (0, 1), (1, 0))):
                    mm = e.matmul(dst[:, cols], w[i][:, cols], x[j][:, cols], start=(a == 0), stop=(a == 2))
            mm.then_inc(inc, 1)

        def chunk_of(t, h):
            return one(t[:, bass.ds(h, 1), :])

        def beta_pe(e):
            e.wait_ge(wb_lo, 1)
            for k in range(KC):
                for a, (w, x) in enumerate(((wbh, xnh), (wbh, xnl), (wbl, xnh))):
                    for c in range(2):
                        mm = e.matmul(bank(4 + c)[0:H, :], w[:, k * H:(k + 1) * H], x[:, k, c * HALF:(c + 1) * HALF],
                                      start=(k == 0 and a == 0), stop=(k == KC - 1 and a == 2))
            mm.then_inc(b_mm, 1)

        def gram_pe(e, h, par):
            e.wait_ge(k_lo, h + 1)
            if isinstance(h, int) and h < 2:
                e.wait_ge(b_sg, 1)
            else:
                e.wait_ge(g_ms, h - 1)
            k = (chunk_of(KH, h), chunk_of(KL, h))
            blocks(e, bank(4 + 2 * par, 2), k, k, g_mm)

        def dk_pe(e):
            def head(h, par, i, last):
                if isinstance(h, int) and h == 0:
                    gemm_pe_ln(e, "dk", 1)
                    beta_pe(e)
                    return
                if not (isinstance(h, int) and h == 1):
                    gemm_pe(e, "dk", h, par, xnh, xnl)
                gram_pe(e, h - 1, 1 - par)
            pairs(e, H, head, peel=2)

        def dk_act(e):
            e.wait_ge(d_ld, 48)
            e.activation(wbh, wbst, ACT.Copy, scale=W_SCALE).then_inc(wb_hi, 1)

            def beta_():
                e.wait_ge(b_mm, 1)
                e.activation(beta, bank(4, 2)[0:H, :], ACT.Sigmoid, scale=1.0 / W_SCALE).then_inc(b_sg, 1)
                e.wait_ge(b_sg, 1)
                e.dma_start(io["beta_s"], beta).then_inc(b_st, 16)

            def store(h, par):
                e.wait_ge(g_c, h + 1)
                e.dma_start(io["gram_s"][bass.ds(h, 1)].rearrange("a g (p j) -> p (a g) j", j=T), gc[par]).then_inc(g_st[par], 16)

            def head(h, par, i, last):
                split_next(e, "hi", "dk", h, par, i)
                conv_act(e, "dk", h, par)
                e.wait_ge(si, h + 1)
                e.activation(chunk_of(KH, h), sv[par], ACT.Copy).then_inc(k_hi, 1)
                if isinstance(h, int) and h == 0:
                    beta_()
                else:
                    store(h - 1, 1 - par)
            pairs(e, H, head, peel=2)
            store(15, 1)

        def dk_dve(e):
            e.wait_ge(wb_hi, 1)
            e.scalar_tensor_tensor(out=wbl, in0=wbst, scalar=W_SCALE, in1=wbh, op0=ALU.mult,
                                   op1=ALU.subtract).then_inc(wb_lo, 1)

            def gram(h, par):
                e.wait_ge(g_mm, h + 1)
                if not (isinstance(h, int) and h < 1):
                    e.wait_ge(g_c, h)
                e.tensor_tensor(gm.rearrange("p (g n) -> p g n", g=G8), bank(4 + 2 * par, 2).rearrange("p (g n) -> p g n", g=G8),
                                bc(same[:, :], G8), ALU.mult).then_inc(g_ms, 1)
                e.wait_ge(g_ms, h + 1)
                if isinstance(h, int):
                    if h >= 2:
                        e.wait_ge(g_st[par], 16 * (h // 2))
                else:
                    e.wait_ge(g_st[par], stored[0])
                e.tensor_reduce(gc[par], gm.rearrange("p (g b j) -> p g j b", g=G8, b=8), AXX, ALU.add).then_inc(g_c, 1)
            stored = [None]

            def head(h, par, i, last):
                split_next(e, "lo", "dk", h, par, i)
                conv_dve(e, "dk", h, par)
                if not (isinstance(h, int) and h == 0):
                    stored[0] = (i - (1 - par)) * 16
                    gram(h - 1, 1 - par)
                e.wait_ge(k_hi, h + 1)
                e.tensor_tensor(chunk_of(KL, h), sv[par], chunk_of(KH, h), ALU.subtract).then_inc(k_lo, 1)
            pairs(e, H, head, peel=2)
            gram(15, 1)

        def solve_pool(e):
            e.wait_ge(d_ld, 48)
            e.wait_ge(b_st, 16)
            for par in range(2):
                e.wait_ge(g_st[par], 128)
            half = lambda t, par: t[64 * par:64 * par + 64]
            for par in range(2):
                e.dma_start(half(sA, par).rearrange("p h i j -> p h (i j)"),
                            io["gram_s"].rearrange("(h a) g (b n) -> a h (g b) n", a=2, b=8)[par].rearrange("h b n -> b h n")).then_inc(seq_ld, 16)
                with nc.allow_non_contiguous_dma(reason="beta by sequence: 64 KiB once"):
                    for h in range(8):
                        e.dma_start(half(betaq, par)[:, h, :],
                                    io["beta_s"].rearrange("(h a) (t b) -> a h b t", a=2, t=T)[par, h]).then_inc(seq_ld, 16)
            e.wait_ge(seq_ld, 16 * 18)
            n = [0]

            def then(ins):
                ins.then_inc(pr, 1)
                n[0] += 1
                e.wait_ge(pr, n[0])
            flat = lambda t: t.rearrange("p h i j -> p h (i j)")
            then(e.memset(nhalf, -0.5))
            then(e.tensor_scalar(rk, flat(sA)[:, :, 0:256:17], 1e-12, None, ALU.add))
            then(e.tensor_tensor(rk, rk, nhalf, ALU.pow))
            then(e.tensor_tensor(rkb, rk, betaq, ALU.mult))
            then(e.tensor_tensor(sA, sA, bc(rkb, T, 3), ALU.mult))
            then(e.tensor_tensor(sA, sA, bc(rk, T, 2), ALU.mult))
            then(e.tensor_tensor(flat(sA), flat(sA), bc(lower.rearrange("p i j -> p (i j)"), 8), ALU.mult))
            e.tensor_copy(flat(sT), bc(eye.rearrange("p i j -> p (i j)"), 8)).then_inc(sl_t, 1)
            with e.Fori(0, T - 1) as j:
                e.wait_ge(sl_t, j + 1)
                e.tensor_tensor(sU, sA[:, :, :, bass.ds(j, 1)].to_broadcast([P, 8, T, T]),
                                sT[:, :, bass.ds(j, 1), :].to_broadcast([P, 8, T, T]), ALU.mult).then_inc(sl_u, 1)
                e.wait_ge(sl_u, j + 1)
                e.tensor_tensor(flat(sT), flat(sT), flat(sU), ALU.subtract).then_inc(sl_t, 1)
            e.wait_ge(sl_t, T)
            then(e.tensor_tensor(sT, sT, bc(rk, T, 3), ALU.mult))
            then(e.tensor_tensor(sT, sT, bc(betaq, T, 2), ALU.mult))
            for par in range(2):
                e.dma_start(io["inv_s"].rearrange("(h a) g (b n) -> a h (g b) n", a=2, b=8)[par].rearrange("h b n -> b h n"),
                            half(sT, par).rearrange("p h i j -> p h (i j)")).then_inc(tc_st, 16)

        def prod_pe(e, h, par):
            e.wait_ge(q_l2, h + 1)
            e.wait_ge(q_sq, h + 1)
            if isinstance(h, int) and h == 0:
                e.wait_ge(g_ms, 16)
            else:
                e.wait_ge(q2_rd, h)
            blocks(e, bank(4, 2), (chunk_of(KH, h), chunk_of(KL, h)), (qdh, qdl), p_mm0)
            for g in range(G8):
                mm = e.matmul(bank(6)[:, par * G8 + g:par * G8 + g + 1],
                              qsq[:, g * P:(g + 1) * P], onesm[:, :], start=True, stop=True)
            mm.then_inc(p_mm, 1)

        def dq_pe(e):
            def head(h, par, i, last):
                gemm_pe(e, "dq", h, par, xnh, xnl)
                if isinstance(h, int) and h == 0:
                    gram_pe(e, 15, 1)
                else:
                    prod_pe(e, h - 1, 1 - par)
            pairs(e, H, head, peel=1)
        p_mm0 = sem("products_alone_ready")

        def dq_act(e):
            def part(h):
                e.wait_ge(p_ms, h + 1)
                e.activation(chunk_of(KH, h), gm, ACT.Copy).then_inc(p_hi, 1)

            def head(h, par, i, last):
                split_next(e, "hi", "dq", h, par, i)
                conv_act(e, "dq", h, par)
                e.wait_ge(si, h + 17)
                if not (isinstance(h, int) and h == 0):
                    e.wait_ge(p_mm, h)
                e.activation(qdh, sv[par], ACT.Copy).then_inc(q_h2, 1)
                e.activation(qsq, sv[par], ACT.Square).then_inc(q_sq, 1)
                if not (isinstance(h, int) and h == 0):
                    part(h - 1)
            pairs(e, H, head, peel=1)
            part(15)

        def dq_dve(e):
            def mask(h, par):
                e.wait_ge(p_mm, h + 1)
                if isinstance(h, int) and h == 0:
                    e.wait_ge(g_c, 16)
                else:
                    e.wait_ge(p_lo, h)
                e.tensor_tensor(gm.rearrange("p (g n) -> p g n", g=G8), bank(4, 2).rearrange("p (g n) -> p g n", g=G8),
                                bc(upto[:, :], G8), ALU.mult).then_inc(p_ms, 1)
                e.tensor_scalar(q2e[:, bass.ds(h * G8, G8)], bank(6)[:, par * G8:(par + 1) * G8], LN_EPS * 128,
                                LN_EPS * 128 * 1e-12, ALU.mult, ALU.add).then_inc(q2_rd, 1)

            def low(h):
                e.wait_ge(p_hi, h + 1)
                e.tensor_tensor(chunk_of(KL, h), gm, chunk_of(KH, h), ALU.subtract).then_inc(p_lo, 1)

            def head(h, par, i, last):
                split_next(e, "lo", "dq", h, par, i)
                conv_dve(e, "dq", h, par)
                if not (isinstance(h, int) and h == 0):
                    mask(h - 1, 1 - par)
                e.wait_ge(q_h2, h + 1)
                e.tensor_tensor(qdl, sv[par], qdh, ALU.subtract).then_inc(q_l2, 1)
                if not (isinstance(h, int) and h == 0):
                    low(h - 1)
            pairs(e, H, head, peel=1)
            mask(15, 1)
            low(15)

        VT = [f16(108 + 2 * k, TOK) for k in range(2)]
        WT = [f16(112 + 2 * k, TOK) for k in range(2)]
        osq, osc = f32(116, TOK), f32(120, TOK)
        tcs = [f32(124 + s / 2, P).rearrange("p (g j) -> p g j", g=G8) for s in range(2)]
        tcp = [[f16(125 + s / 2 + k / 4, P).rearrange("p (g j) -> p g j", g=G8) for k in range(2)] for s in range(2)]
        TB = [[f16(128 + 4 * s + 2 * k, TOK) for k in range(2)] for s in range(2)]
        same16 = f16(136, P)
        osum, ofac, otmp = small[:, 16:24], small[:, 24:32], small[:, 32:40]
        nh8 = small[:, 40:48]
        tc_ld = [sem("inverse_loaded_0"), sem("inverse_loaded_1")]
        v_c = sem("value_constants")
        tb_c = sem("inverse_parts")
        tb_d = sem("inverse_blocks")
        vt_mm = sem("values_turned")
        vt_hi = sem("values_turned_hi")
        vt_lo = sem("values_turned_split")
        wt_mm = sem("delta_weights_ready")
        wt_hi = sem("delta_weights_hi")
        wt_lo = sem("delta_weights_split")
        o_mm = sem("delta_output_ready")
        o_sq = sem("delta_output_square")
        o_sm = sem("delta_output_square_sum")
        o_ms = sem("delta_output_mean_square")
        o_fc = sem("delta_output_factor")
        o_sc = sem("delta_output_scaled")
        ot_mm = sem("delta_output_turned")
        ot_hi = sem("delta_output_hi")
        ot_lo = sem("delta_output_split")

        def dv_sp(e, u0):
            def tc(h, s):
                e.dma_start(tcs[s], io["inv_s"][bass.ds(h, 1)].rearrange("a g (p j) -> p (a g) j", j=T)).then_inc(tc_ld[s], 16)
            e.wait_ge(tc_st, 32)
            e.wait_ge(q2_rd, 16)
            tc(0, 0)
            tc(1, 1)
            with e.Fori(1, 8) as i:
                for s in range(2):
                    e.wait_ge(w_rdy, i * 2 + (u0 - 2 + s - 1))
                    load_w(e, i * 2 + (u0 - 2 + s), s)
                    e.wait_ge(tb_c, i * 2 + (s - 1))
                    tc(i * 2 + s, s)

        def steps(e, body):
            for h in range(2):
                body(h, h % 2, h // 2)
            with e.Fori(1, 8) as i:
                for par in range(2):
                    body(i * 2 + par, par, i)
            for h in (16, 17):
                body(h, h % 2, h // 2)

        def has(h, back):
            return not isinstance(h, int) or 0 <= h - back < H

        def dv_pe(e):
            def do_first(q, k0, k1):
                if q == 0 and k0 == 0:
                    e.wait_ge(acc_rd, ACC0["do"] + 1)
                e.wait_ge(w_rdy, UNIT0["do"] + q + 1)
                e.wait_ge(ot_lo, 8 * q + k1)
                unit_mm(e, q, bank(0, 2), KH, KL, q * 8, range(k0, k1), q == 0 and k0 == 0, q == 1 and k1 == 8, k1 == 8)

            def step(h, par, i):
                if has(h, 0):
                    gemm_pe(e, "dv", h, par, xnh, xnl, parts=(0, 4))
                    if isinstance(h, int) and h == 0:
                        prod_pe(e, 15, 1)
                elif h == 16:
                    do_first(0, 0, 4)
                else:
                    do_first(1, 0, 6)
                if has(h, 2):
                    e.wait_ge(o_sc, h - 1)
                    if has(h, 1):
                        e.wait_ge(wt_lo, h)
                    for g in range(G8):
                        mm = e.transpose(bank(6, 2)[:, g * P:(g + 1) * P], osc[:, g * P:(g + 1) * P], xid[:, :])
                    mm.then_inc(ot_mm, 1)
                if has(h, 0):
                    gemm_pe(e, "dv", h, par, xnh, xnl, parts=(4, 6))
                elif h == 16:
                    do_first(0, 4, 6)
                if has(h, 1):
                    e.wait_ge(si, h + 32)
                    if has(h, 2):
                        e.wait_ge(o_sc, h - 1)
                    for g in range(G8):
                        mm = e.transpose(bank(4, 2)[:, g * P:(g + 1) * P], sv[1 - par][:, g * P:(g + 1) * P], xid[:, :])
                    mm.then_inc(vt_mm, 1)
                if has(h, 0):
                    gemm_pe(e, "dv", h, par, xnh, xnl, parts=(6, 8))
                elif h == 16:
                    do_first(0, 6, 8)
                if has(h, 1):
                    e.wait_ge(vt_lo, h)
                    e.wait_ge(wt_lo, h)
                    blocks(e, bank(4, 2), WT, VT, o_mm)
                if has(h, 0):
                    if isinstance(h, int) and h == 0:
                        e.wait_ge(q2_rd, 16)
                        e.wait_ge(p_lo, 16)
                    e.wait_ge(tb_d, h + 1)
                    if has(h, 2):
                        e.wait_ge(ot_lo, h - 1)
                    blocks(e, bank(6, 2), TB[par], (chunk_of(KH, h), chunk_of(KL, h)), wt_mm)
            steps(e, step)
            for k in (6, 7):
                do_first(1, k, k + 1)

        def turned(t):
            return t.rearrange("p (b t) -> p t b", t=T)

        def straight(t):
            return t.rearrange("p (t b) -> p t b", t=T)

        def dv_act(e):
            def step(h, par, i):
                if has(h, 2):
                    e.wait_ge(o_mm, h - 1)
                    e.activation(osq, bank(4, 2), ACT.Square).then_inc(o_sq, 1)
                if has(h, 1):
                    e.wait_ge(wt_mm, h)
                    e.activation(WT[0], bank(6, 2), ACT.Copy).then_inc(wt_hi, 1)
                def turned_output():
                    if has(h, 2):
                        e.wait_ge(ot_mm, h - 1)
                        e.activation(straight(chunk_of(KH, h - 2)), turned(bank(6, 2)), ACT.Copy, scale=gno).then_inc(ot_hi, 1)
                if has(h, 1):
                    conv_act(e, "dv", h - 1, 1 - par, turned_output)
                    e.wait_ge(vt_mm, h)
                    e.activation(VT[0], bank(4, 2), ACT.Copy).then_inc(vt_hi, 1)
                else:
                    turned_output()
                if has(h, 0):
                    split_next(e, "hi", "dv", h, par, i)
            steps(e, step)

        def dv_dve(e):
            def step(h, par, i):
                if has(h, 2):
                    e.wait_ge(o_sq, h - 1)
                    e.tensor_reduce(osum, osq.rearrange("p (g d) -> p g d", g=G8), AXX, ALU.add).then_inc(o_sm, 1)
                    e.wait_ge(o_sm, h - 1)
                    e.scalar_tensor_tensor(out=otmp, in0=osum, scalar=1.0 / P,
                                           in1=q2e[:, bass.ds((h - 2) * G8, G8)] if not isinstance(h, int) else q2e[:, (h - 2) * G8:(h - 1) * G8],
                                           op0=ALU.mult, op1=ALU.add).then_inc(o_ms, 1)
                if has(h, 1):
                    e.wait_ge(wt_hi, h)
                    e.tensor_tensor(WT[1], bank(6, 2), WT[0], ALU.subtract).then_inc(wt_lo, 1)
                if has(h, 2):
                    e.wait_ge(o_fc, h - 1)
                    e.tensor_tensor(osc.rearrange("p (g d) -> p g d", g=G8), bank(4, 2).rearrange("p (g d) -> p g d", g=G8),
                                    bc(ofac, P, 2), ALU.mult).then_inc(o_sc, 1)
                if has(h, 1):
                    conv_dve(e, "dv", h - 1, 1 - par)
                if has(h, 2):
                    e.wait_ge(ot_hi, h - 1)
                    e.scalar_tensor_tensor(out=straight(chunk_of(KL, h - 2)), in0=turned(bank(6, 2)), scalar=gno,
                                           in1=straight(chunk_of(KH, h - 2)), op0=ALU.mult, op1=ALU.subtract).then_inc(ot_lo, 1)
                if has(h, 1):
                    e.wait_ge(vt_hi, h)
                    e.tensor_tensor(VT[1], bank(4, 2), VT[0], ALU.subtract).then_inc(vt_lo, 1)
                if has(h, 0):
                    split_next(e, "lo", "dv", h, par, i)
            steps(e, step)

        def dv_pool(e):
            e.wait_ge(tc_st, 32)
            e.wait_ge(q2_rd, 16)
            e.tensor_copy(same16, same[:, :]).then_inc(v_c, 1)
            e.memset(nh8, -0.5).then_inc(v_c, 1)
            e.wait_ge(v_c, 2)

            def step(h, par, i):
                if has(h, 2):
                    e.wait_ge(o_ms, h - 1)
                    e.tensor_tensor(ofac, otmp, nh8, ALU.pow).then_inc(o_fc, 1)
                if has(h, 0):
                    e.wait_ge(tc_ld[par], (i + 1) * 16)
                    e.tensor_tensor(tcp[par][0], tcs[par], onesm[:, :].unsqueeze(2).to_broadcast([P, G8, T]),
                                    ALU.mult).then_inc(tb_h, 1)
                    e.wait_ge(tb_h, h + 1)
                    e.tensor_tensor(tcp[par][1], tcs[par], tcp[par][0], ALU.subtract).then_inc(tb_c, 1)
                    e.wait_ge(tb_c, h + 1)
                    if has(h, 2):
                        e.wait_ge(wt_mm, h - 1)
                    for k in range(2):
                        ins = e.tensor_tensor(TB[par][k].rearrange("p (g b j) -> p g b j", g=G8, b=8),
                                              bc(tcp[par][k], 8, 2),
                                              bc(same16.rearrange("p (b j) -> p b j", b=8), G8), ALU.mult)
                    ins.then_inc(tb_d, 1)
            steps(e, step)
        tb_h = sem("inverse_parts_hi")

        h2h, h2l = f16c(64, 16), f16c(96, 16)
        rb = [f32(128 + 4 * s, TOK) for s in range(2)]
        f_r = sem("hidden_chunk")
        f_hi = sem("hidden_hi")
        od = [sem("output_stored_0"), sem("output_stored_1")]
        FB = {"f1": 0, "f2": 16, "f3": 32}

        def hidden_pe(e, name, sh, sl):
            def chunk(m, par, i, last):
                if name == "f1" and isinstance(m, int) and m < 2:
                    if m == 0:
                        gemm_pe_ln(e, "f1", 2)
                elif name == "f2" and isinstance(m, int) and m == 0:
                    gemm_pe_first(e, "f2", "f1", sh, sl)
                else:
                    gemm_pe(e, name, m, par, sh, sl)
            pairs(e, H, chunk, peel=1)

        def hidden_act(e, name, bias, dst):
            def chunk(m, par, i, last):
                split_next(e, "hi", name, m, par, i)
                e.wait_ge(w_used, used(name, m))
                e.wait_ge(acc_rd, m + (ACC0[name] + 1))
                e.activation(rb[par], bank(2 * par, 2), ACT.Relu, bias=bias[:, bass.ds(m, 1)],
                             scale=1.0 / W_SCALE).then_inc(f_r, 1)
                e.wait_ge(f_r, m + (FB[name] + 1))
                e.activation(chunk_of(dst, m), rb[par], ACT.Copy).then_inc(f_hi, 1)
            pairs(e, H, chunk)

        def hidden_dve(e, name, dsth, dstl):
            def chunk(m, par, i, last):
                split_next(e, "lo", name, m, par, i)
                e.wait_ge(f_hi, m + (FB[name] + 1))
                e.tensor_tensor(chunk_of(dstl, m), rb[par], chunk_of(dsth, m), ALU.subtract).then_inc(acc_rd, 1)
            pairs(e, H, chunk)

        def out_pe(e):
            def chunk(m, par, i, last):
                if isinstance(m, int) and m == 0:
                    gemm_pe_first(e, "f3", "f2", h2h, h2l)
                else:
                    gemm_pe(e, "f3", m, par, h2h, h2l)
            pairs(e, KC, chunk, peel=1)

        def out_act(e):
            def chunk(m, par, i, last):
                if not (last and par):
                    split_next(e, "hi", "f3", m, par, i)
                e.wait_ge(w_used, used("f3", m))
                e.wait_ge(acc_rd, m + (ACC0["f3"] + 1))
                if not (isinstance(m, int) and m < 2):
                    e.wait_ge(od[par], i * 16)
                e.activation(rb[par], bank(2 * par, 2), ACT.Identity, bias=b3c[:, bass.ds(m, 1)],
                             scale=1.0 / W_SCALE).then_inc(f_r, 1)
            pairs(e, KC, chunk, peel=1, peel_end=1)

        def out_dve(e):
            def chunk(m, par, i, last):
                if not (last and par):
                    split_next(e, "lo", "f3", m, par, i)
                e.wait_ge(f_r, m + (FB["f3"] + 1))
                e.tensor_tensor(rb[par], rb[par], x_chunk(m), ALU.add).then_inc(acc_rd, 1)
            pairs(e, KC, chunk, peel_end=1)

        def out_sp(e):
            u0 = UNIT0["f3"] + 2

            def chunk(m, par, i, last):
                if not (last and par):
                    for q in range(2):
                        e.wait_ge(w_rdy, m * 2 + (u0 + q - 1))
                        load_w(e, m * 2 + (u0 + q), q)
                e.wait_ge(acc_rd, acc_done("f3", m))
                e.dma_start(io["out"][:, bass.ds(m, 1), :].rearrange("p a n -> p (a n)"), rb[par]).then_inc(od[par], 16)
            pairs(e, KC, chunk, peel_end=1)
            for s in range(2):
                e.wait_ge(od[s], 64)

        block = ctx.enter_context(nc.Block())

        @block.sync
        def _(sp):
            start_sp(sp)
            xa_sp(sp)
            xb_sp(sp)
            xo_sp(sp)
            load_stream(sp, 18, UNIT0["dv"] + 2)
            dv_sp(sp, UNIT0["dv"] + 2)
            load_stream(sp, UNIT0["dv"] + 16, UNIT0["f3"] + 2)
            out_sp(sp)

        @block.tensor
        def _(pe):
            start_pe(pe)
            xa_pe(pe)
            xb_pe(pe)
            pe.wait_ge(cl_lo, 32)
            residual_pe(pe, "xo", 1, QR, QRL)
            dk_pe(pe)
            dq_pe(pe)
            dv_pe(pe)
            residual_pe(pe, "do", 2, KH, KL)
            hidden_pe(pe, "f1", xnh, xnl)
            hidden_pe(pe, "f2", r0h, r0l)
            out_pe(pe)

        @block.scalar
        def _(act):
            start_act(act)
            xa_act(act)
            xb_act(act)
            act.wait_ge(xr_ld, 16)
            residual_act(act, "xo", 1)
            dk_act(act)
            dq_act(act)
            dv_act(act)
            residual_act(act, "do", 2)
            hidden_act(act, "f1", b1c, r0h)
            hidden_act(act, "f2", b2c, h2h)
            out_act(act)

        @block.vector
        def _(dve):
            start_dve(dve)
            xa_dve(dve)
            xb_dve(dve)
            dve.wait_ge(xr_ld, 16)
            residual_dve(dve, "xo", 1)
            dk_dve(dve)
            dq_dve(dve)
            dv_dve(dve)
            residual_dve(dve, "do", 2)
            hidden_dve(dve, "f1", r0h, r0l)
            hidden_dve(dve, "f2", h2h, h2l)
            out_dve(dve)

        @block.gpsimd
        def _(pool):
            start_pool(pool)
            xa_pool(pool)
            xb_pool(pool)
            pool.wait_ge(xr_ld, 16)
            residual_pool(pool, "xo", 1)
            solve_pool(pool)
            dv_pool(pool)
            pool.wait_ge(ot_lo, 16)
            residual_pool(pool, "do", 2)


def _layouts(inputs):
    import numpy as np

    def a(name):
        return np.ascontiguousarray(inputs[name])

    def units(w):
        o, i = w.shape
        return w.reshape(o // P, P, i // 1024, 8, P).transpose(0, 2, 4, 3, 1).reshape(-1, P, 1024)

    t = np.float32
    out = {}
    out["xT"] = a("x").reshape(TOK, KC, P).transpose(2, 1, 0)
    out["wstream"] = np.concatenate([
        units(a("L0_xattn_Wq")), units(a("L0_xattn_Wo")), units(a("L0_attn_Wk").T), units(a("L0_attn_Wq").T),
        units(a("L0_attn_Wv").T), units(a("L0_attn_Wo").T), units(a("L0_ffn_W1")), units(a("L0_ffn_W2")),
        units(a("L0_ffn_W3"))])
    wqr = a("L0_xattn_W_qr").reshape(H, CJ, P, R).transpose(0, 2, 1, 3).reshape(H, P, CJ * R)
    out["abstream"] = np.concatenate([a("L0_xattn_w_kc_q"), wqr], axis=2)
    wkr = a("L0_xattn_W_kr").transpose(2, 0, 1)
    wkv = a("L0_xattn_w_kc_kv").reshape(H, P, 2, P).transpose(3, 0, 2, 1)
    out["wk"] = np.stack([np.concatenate([wkr, wkr]).reshape(P, H * DC), wkv.reshape(P, H * DC)])
    c = a("ctx_512")
    out["ctx"] = np.stack([c.reshape(NB, L, 2, P).transpose(0, 3, 2, 1).reshape(NB, P, TOK),
                           c.reshape(NB, 4, P, DC).transpose(0, 2, 1, 3).reshape(NB, P, TOK)])

    def rope(length, dim):
        inv = t(1.0) / t(10000.0) ** (np.arange(0, dim, 2, dtype=t) / t(dim))
        f = np.arange(length, dtype=t)[:, None] * inv[None, :]
        sin, cos = np.repeat(np.sin(f), 2, axis=-1), np.repeat(np.cos(f), 2, axis=-1)
        sign = np.where(np.arange(dim) < dim // 2, t(-1), t(1))
        return (sin * sign).astype(t), cos.astype(t)
    for name, tab in zip(("rsin", "rcos"), rope(S, CQ)):
        out[name] = (tab * t(1.0 / W_SCALE)).T.reshape(CJ, P, S).transpose(1, 0, 2)
    for name, tab in zip(("ksin", "kcos"), rope(L, DC)):
        out[name] = np.stack([tab.T.reshape(2, P, L).transpose(1, 0, 2).reshape(P, TOK),
                              tab.reshape(4, P, DC).transpose(1, 0, 2).reshape(P, TOK)])
    v = np.zeros((P, 256), t)
    v[:, 0:16] = a("L0_ffn_b1").reshape(16, P).T
    v[:, 16:32] = a("L0_ffn_b2").reshape(16, P).T
    v[:, 32:40] = a("L0_ffn_b3").reshape(8, P).T
    v[:, 40] = a("L0_attn_g_norm")
    for k, n in enumerate(("k", "q", "v")):
        v[:, 48 + 64 * k:112 + 64 * k] = a(f"L0_attn_conv_{n}").reshape(H, P, 4).transpose(1, 0, 2).reshape(P, 64)
    out["vecs"] = v
    out["wb"] = a("L0_attn_Wb").reshape(KC, P, H).transpose(1, 0, 2).reshape(P, P)
    seq, step = np.arange(P) // T, np.arange(P) % T
    out["ident"] = np.eye(P, dtype=t)
    out["ones"] = np.full((P, P), 1.0 / DM, t)
    out["same"] = (seq[:, None] == seq[None, :]).astype(t)
    out["upto"] = out["same"] * (step[:, None] <= step[None, :])
    out["lower"] = np.broadcast_to(np.tril(np.ones((T, T), t), -1)[None], (P, T, T))
    out["eye"] = np.broadcast_to(np.eye(T, dtype=t)[None], (P, T, T))
    return {k: np.ascontiguousarray(x.astype(t)) for k, x in out.items()}


def kernel(**inputs):
    import numpy as np
    import concourse.bacc as bacc
    from concourse.bass_utils import run_bass_kernel_spmd

    nc = bacc.Bacc("TRN2", target_bir_lowering=False, num_devices=1)
    arrays = _layouts(inputs)
    io = {n: nc.dram_tensor(n, x.shape, F32, kind="ExternalInput").ap() for n, x in arrays.items()}
    io["beta_s"] = nc.dram_tensor("beta_s", (H, TOK), F32, kind="Internal").ap()
    io["gram_s"] = nc.dram_tensor("gram_s", (H, G8, 8 * T * T), F32, kind="Internal").ap()
    io["inv_s"] = nc.dram_tensor("inv_s", (H, G8, 8 * T * T), F32, kind="Internal").ap()
    io["out"] = nc.dram_tensor("out", (P, KC, TOK), F32, kind="ExternalOutput").ap()
    build(nc, io)
    got = run_bass_kernel_spmd(nc, [arrays], core_ids=[0]).results[0]["out"]
    return np.ascontiguousarray(got.transpose(2, 1, 0)).reshape(16, 64, DM)
```
